# Optimizing a Trainium2 kernel written in Bass

```python
import numpy as np
import jax
import jax.numpy as jnp

def _softmax(x, axis=-1):
    return jax.nn.softmax(x, axis=axis)

def _gelu(x):
    return jax.nn.gelu(x, approximate=True)

def _silu(x):
    return jax.nn.silu(x)

def _sigmoid(x):
    return jax.nn.sigmoid(x)

def _layernorm(x, axis=-1, eps=1e-05):
    m = jnp.mean(x, axis=axis, keepdims=True)
    v = jnp.var(x, axis=axis, keepdims=True)
    return (x - m) / jnp.sqrt(v + eps)

def _scatter_add(tgt, idx, src, axis=0):
    return tgt.at[idx].add(src)

def _segment_sum(src, seg, n):
    return jax.ops.segment_sum(src, seg, n)
kernel_name = 'mk_conv_attn_hybrid_d2_conv_nchw128_r2_171883'

def setup_inputs(seed: int=0):
    np.random.seed(seed)
    _w = jnp.asarray

    def _rec_inputs():
        import jax
        import jax.numpy as jnp
        _gk = jax.random.key(seed)
        x = -0.0005207 + 1.001 * jax.random.normal(jax.random.fold_in(_gk, 1), (4, 64, 32, 32), jnp.float32)
        return x
    x = _rec_inputs()

    def _L0_conv_setup():
        import jax, jax.numpy as jnp
        import numpy as np
        B, C, H, W = (4, 64, 32, 32)
        MEDIA_C = 32
        key = jax.random.key(seed)
        ks = jax.random.split(key, 5)
        return {'x': jax.random.normal(ks[0], (B, C, H, W), dtype=jnp.float32), 'wq': jax.random.normal(ks[1], (MEDIA_C, C), dtype=jnp.float32) * (1.0 / np.sqrt(C)), 'wk': jax.random.normal(ks[2], (MEDIA_C, C), dtype=jnp.float32) * (1.0 / np.sqrt(C)), 'wv': jax.random.normal(ks[3], (MEDIA_C, C), dtype=jnp.float32) * (1.0 / np.sqrt(C)), 'wo': jax.random.normal(ks[4], (C, MEDIA_C), dtype=jnp.float32) * (1.0 / np.sqrt(MEDIA_C))}
    _L0_conv_all = _L0_conv_setup()
    _L0_conv_in = {k: v for k, v in _L0_conv_all.items() if k in ('wq', 'wk', 'wv', 'wo')}
    del _L0_conv_all

    def _L1_attn_setup():
        import jax, jax.numpy as jnp
        import numpy as np
        NEG_INF = -1e+30
        key = jax.random.key(seed)
        ks = jax.random.split(key, 5)
        B, N, D, H = (4, 1024, 64, 8)
        scale = 0.02
        return {'x': jax.random.normal(ks[0], (B, N, D), dtype=jnp.float32), 'Wq': jax.random.normal(ks[1], (D, D * H), dtype=jnp.float32) * scale, 'Wk': jax.random.normal(ks[2], (D, D * H), dtype=jnp.float32) * scale, 'Wv': jax.random.normal(ks[3], (D, D * H), dtype=jnp.float32) * scale, 'Wo': jax.random.normal(ks[4], (D * H, D), dtype=jnp.float32) * scale}
    _L1_attn_all = _L1_attn_setup()
    _L1_attn_in = {k: v for k, v in _L1_attn_all.items() if k in ('Wq', 'Wk', 'Wv', 'Wo')}
    del _L1_attn_all

    def _L1_ffn_setup():
        import jax, jax.numpy as jnp
        import numpy as np
        BN_EPS = 1e-05
        key = jax.random.key(seed)
        k1, k2, k3 = jax.random.split(key, 3)
        B, T, I, H = (32, 1024, 64, 64)
        x = jax.random.normal(k1, (B, T, I), dtype=jnp.float32)
        W = jax.random.normal(k2, (H, I), dtype=jnp.float32) * (1.0 / np.sqrt(I))
        V = jnp.linalg.qr(jax.random.normal(k3, (H, H), dtype=jnp.float32))[0]
        gamma = jnp.ones((H,), dtype=jnp.float32)
        beta = jnp.zeros((H,), dtype=jnp.float32)
        return {'x': x, 'W': W, 'V': V, 'gamma': gamma, 'beta': beta}
    _L1_ffn_all = _L1_ffn_setup()
    _L1_ffn_in = {k: v for k, v in _L1_ffn_all.items() if k in ('W', 'V', 'gamma', 'beta')}
    del _L1_ffn_all
    return {'x': x, 'L0_conv_wq': _L0_conv_in['wq'], 'L0_conv_wk': _L0_conv_in['wk'], 'L0_conv_wv': _L0_conv_in['wv'], 'L0_conv_wo': _L0_conv_in['wo'], 'L1_attn_Wq': _L1_attn_in['Wq'], 'L1_attn_Wk': _L1_attn_in['Wk'], 'L1_attn_Wv': _L1_attn_in['Wv'], 'L1_attn_Wo': _L1_attn_in['Wo'], 'L1_ffn_W': _L1_ffn_in['W'], 'L1_ffn_V': _L1_ffn_in['V'], 'L1_ffn_gamma': _L1_ffn_in['gamma'], 'L1_ffn_beta': _L1_ffn_in['beta']}

def reference(x, L0_conv_wq, L0_conv_wk, L0_conv_wv, L0_conv_wo, L1_attn_Wq, L1_attn_Wk, L1_attn_Wv, L1_attn_Wo, L1_ffn_W, L1_ffn_V, L1_ffn_gamma, L1_ffn_beta):
    import jax
    import jax.numpy as jnp

    def _L0_conv_ref(x, wq, wk, wv, wo):
        import jax, jax.numpy as jnp
        import numpy as np
        B, C, H, W = (4, 64, 32, 32)
        MEDIA_C = 32
        b, c, h, w = x.shape
        n = h * w
        xf = x.reshape(b, c, n)
        q = jnp.einsum('mc,bcn->bmn', wq, xf)
        k = jnp.einsum('mc,bcn->bmn', wk, xf)
        v = jnp.einsum('mc,bcn->bmn', wv, xf)
        att = jnp.einsum('bmi,bmj->bij', k, q)
        att = jax.nn.softmax(att, axis=2)
        agg = jnp.einsum('bij,bmj->bmi', att, v)
        out = x + jnp.einsum('cm,bmn->bcn', wo, agg).reshape(b, c, h, w)
        return out

    def _L1_attn_ref(x, Wq, Wk, Wv, Wo):
        import jax, jax.numpy as jnp
        import numpy as np
        NEG_INF = -1e+30
        B, N, D = x.shape
        H = Wq.shape[1] // D
        q = (x @ Wq).reshape(B, N, H, D).transpose(0, 2, 1, 3)
        k = (x @ Wk).reshape(B, N, H, D).transpose(0, 2, 1, 3)
        v = (x @ Wv).reshape(B, N, H, D).transpose(0, 2, 1, 3)
        scores = jnp.einsum('bhqd,bhkd->bhqk', q, k) / D ** 0.5
        causal = jnp.triu(jnp.ones((N, N), dtype=bool), k=1)
        scores = jnp.where(causal[None, None], NEG_INF, scores)
        attn = jax.nn.softmax(scores, axis=-1)
        out = jnp.einsum('bhqk,bhkd->bhqd', attn, v)
        out = out.transpose(0, 2, 1, 3).reshape(B, N, H * D)
        return out @ Wo

    def _L1_ffn_ref(x, W, V, gamma, beta):
        import jax, jax.numpy as jnp
        import numpy as np
        BN_EPS = 1e-05
        B, T, H = (x.shape[0], x.shape[1], W.shape[0])
        Wx = jnp.einsum('bti,hi->bth', x, W)
        flat = Wx.reshape(B * T, H)
        mean = jnp.mean(flat, axis=0)
        var = jnp.var(flat, axis=0)
        Wx = ((flat - mean) * jax.lax.rsqrt(var + BN_EPS) * gamma + beta).reshape(B, T, H)
        Vt = V.T

        def step(yt, wx_t):
            yt = jax.nn.sigmoid(wx_t + yt @ Vt)
            return (yt, yt)
        y0 = jnp.zeros((B, H), dtype=Wx.dtype)
        _, ys = jax.lax.scan(step, y0, jnp.swapaxes(Wx, 0, 1))
        return jnp.swapaxes(ys, 0, 1)

    def _gn(v, G=32, eps=1e-05):
        B_, C_, H_, W_ = v.shape
        g = v.reshape(B_, G, C_ // G, H_, W_)
        m = jnp.mean(g, axis=(2, 3, 4), keepdims=True)
        s = jnp.var(g, axis=(2, 3, 4), keepdims=True)
        return ((g - m) / jnp.sqrt(s + eps)).reshape(v.shape)

    def _ln_c(v, eps=1e-06):
        m = jnp.mean(v, axis=1, keepdims=True)
        s = jnp.var(v, axis=1, keepdims=True)
        return (v - m) / jnp.sqrt(s + eps)

    def _ln_t(v, eps=1e-05):
        m = jnp.mean(v, axis=-1, keepdims=True)
        s = jnp.var(v, axis=-1, keepdims=True)
        return (v - m) / jnp.sqrt(s + eps)

    def _to_tokens(v):
        B_, C_, H_, W_ = v.shape
        return v.reshape(B_, C_, H_ * W_).transpose(0, 2, 1)

    def _from_tokens(t, like):
        B_, C_, H_, W_ = like.shape
        return t.transpose(0, 2, 1).reshape(B_, C_, H_, W_)
    x = _L0_conv_ref(x, L0_conv_wq, L0_conv_wk, L0_conv_wv, L0_conv_wo)
    t = _to_tokens(x)
    t = t + _L1_attn_ref(_ln_t(t), L1_attn_Wq, L1_attn_Wk, L1_attn_Wv, L1_attn_Wo)
    t = t + _L1_ffn_ref(_ln_t(t), L1_ffn_W, L1_ffn_V, L1_ffn_gamma, L1_ffn_beta)
    x = _from_tokens(t, x)
    return x

_drawn_inputs = setup_inputs


def setup_inputs(seed=0):
    import zlib

    import numpy as np

    out = dict(_drawn_inputs(seed))
    spreads = {'L1_ffn_gamma': (1.0, 0.6), 'L1_ffn_beta': (0.0, 0.569)}
    factors = {'L1_attn_Wq': 8.0, 'L1_attn_Wk': 8.0, 'L1_attn_Wv': 8.0, 'L1_attn_Wo': 8.0}
    for name, (base, spread) in spreads.items():
        noise = np.random.default_rng([zlib.crc32(name.encode()), seed]).standard_normal(out[name].shape)
        drawn = base * np.exp(spread * noise) if base else spread * noise
        out[name] = jnp.asarray(drawn.astype(out[name].dtype))
    for name, factor in factors.items():
        out[name] = (out[name] * factor).astype(out[name].dtype)
    return out
```

```python
import concourse.bass as bass
from concourse import mybir
from contextlib import ExitStack

B, C, N = 4, 64, 1024
MC = 32
H, D = 8, 64
P = 128
NT = N // P
CW = 512
NC = N // CW
TPC = CW // P
UNITS = B * H
PO = C + 1

ST_RING, MX_RING, P_RING, E_RING = 3, 2, 12, 6
REST_LAG = 3
LAG = 5

HALF_SWEEPS = 4
FULL_SWEEPS = 7
RESIDUAL_LIMIT = 2.0 ** -21

K_IDENT, K_AVG, K_MASK_T, K_MASK_R, K_DIFF = 0, 128, 256, 384, 512
CONST_COLS = 640
NEG = -1e30


class Sems:

    def __init__(self, sem, tag):
        self.scores = sem(f"{tag}_scores_in_psum")
        self.probs32 = sem(f"{tag}_probs32_written")
        self.probs = sem(f"{tag}_probs_written")
        self.rest_pool = sem(f"{tag}_rest_by_pool")
        self.rest_dve = sem(f"{tag}_rest_by_dve")
        self.values = sem(f"{tag}_values_accumulated")
        self.zcopied = sem(f"{tag}_z_copied")
        self.projected = sem(f"{tag}_chunk_projected")
        self.recip = sem(f"{tag}_recip")
        self.added = sem(f"{tag}_chunk_added")
        self.prep = sem(f"{tag}_prep_in_psum")
        self.prep_used = sem(f"{tag}_prep_used")
        self.cast = sem(f"{tag}_high_part_cast")
        self.rowmax = sem(f"{tag}_row_max")
        self.maxrow = sem(f"{tag}_max_row_dma")


class Phase:

    def __init__(self, causal, prep, dve_items):
        self.causal = causal
        self.items = []
        for c in range(NC):
            for j in range(TPC * (c + 1) if causal else NT):
                off = max(0, (j - TPC * c)) * P if causal else 0
                self.items.append((c, j, off, causal and j >= TPC * c))
        self.n = len(self.items)
        self.last = [max(i for i, it in enumerate(self.items) if it[0] == c) for c in range(NC)]
        self.first = [min(i for i, it in enumerate(self.items) if it[0] == c) for c in range(NC)]
        self.maxes = []
        for t in range(NT):
            keys = (t + 1) * P if causal else N
            for part in range((keys + CW - 1) // CW):
                k0 = part * CW
                w = min(CW, keys - k0)
                self.maxes.append((t, part, k0, w, causal and k0 + w == keys))
        self.prep = prep
        self.nprep = prep + len(self.maxes) + 1
        self.dve_items = sorted(dve_items)
        self.pool_items = [i for i in range(self.n) if i not in dve_items]

    def rest_wait(self, s, u, n):
        if n in self.dve_items:
            return s.rest_dve, u * len(self.dve_items) + self.dve_items.index(n) + 1
        return s.rest_pool, u * len(self.pool_items) + self.pool_items.index(n) + 1

    def back(self, u, n, k):
        return (u, n - k) if n >= k else (u - 1, n - k + self.n)


def build(nc, x_cm, x_tm, conv_w, conv_proj, w_q, w_k, w_v, w_o, ffn, gb, const, out):
    f32, f16, bf16, i32 = mybir.dt.float32, mybir.dt.float16, mybir.dt.bfloat16, mybir.dt.int32
    ALU, ACT, AX = mybir.AluOpType, mybir.ActivationFunctionType, mybir.AxisListType.X
    ds = bass.ds

    CONV = Phase(causal=False, prep=6, dve_items={1, 4, 7, 10, 13})
    ATTN = Phase(causal=True, prep=2, dve_items={2, 6, 10})
    SCALE = float(D) ** -0.5

    ctx = ExitStack()
    with ctx:
        def sb(name, shape, dt=f32):
            return ctx.enter_context(nc.sbuf_tensor(name, shape, dt))

        def sem(name):
            return ctx.enter_context(nc.semaphore(name))

        xc = sb("x_channels", [C, B * N])
        tok = sb("tokens", [P, NT * B * C])
        cw = sb("conv_weights", [C, 3 * P])
        cproj = sb("conv_projection", [P, PO])
        wq = sb("w_q", [C, H * D])
        wk = sb("w_k", [C, H * D])
        wv = sb("w_v", [C, H * D])
        wo = sb("w_o", [P, H // 2, C])
        ffn_w = sb("ffn_weights", [P, 2, P])
        gbt = sb("gamma_beta", [P, 2])
        cst = sb("constants", [P, CONST_COLS])
        ident16 = sb("identity_fp16", [P, P], f16)
        identbf = sb("identity_bf16", [P, P], bf16)
        masks = sb("causal_masks", [P, 2, P], bf16)
        wqT = sb("wq_pairs_T", [P, H // 2, P])
        wkT = sb("wk_pairs_T", [P, H // 2, P])
        wvT = sb("wv_pairs_T", [P, H // 2, P])
        a_hi = sb("qk_matrix_high", [P, H * P], f16)
        a_lo = sb("qk_matrix_low", [P, H * P], f16)
        proj = sb("attn_projection", [P, H * PO])
        cxs = sb("conv_keys", [P, B * N], f16)
        cxt = sb("conv_values", [P, B * NT * P], f16)
        xs = sb("attn_keys", [P, B * N], f16)
        xt = sb("attn_values", [P, B * NT * P], f16)
        q_hi = [sb(f"queries_high{i}", [P, N], f16) for i in range(2)]
        q_lo = [sb(f"queries_low{i}", [P, N], f16) for i in range(2)]
        e32 = sb("probs32", [P, E_RING, CW])
        p_hi = sb("probs_high", [P, P_RING, CW], f16)
        p_lo = sb("probs_low", [P, P_RING, CW], f16)
        zs = sb("z", [P, NC, CW])
        rden = sb("reciprocal_denominators", [P, NC, TPC])
        cmx = [sb(f"conv_partial_max{i}", [P, NT, NC]) for i in range(2)]
        amx = [sb(f"attn_partial_max{i}", [P, NT, NC]) for i in range(2)]
        m8 = [sb(f"row_max{i}", [P, NT]) for i in range(2)]
        mrow = [sb(f"minus_max_rows{i}", [NT, P], f16) for i in range(2)]
        stats = sb("ln_stats", [P, NT, 6])
        mv = sb("ln_mean_var", [P, NT, 2])
        rstd = sb("ln_rstd", [P, NT])
        nwt = sb("newton_scratch", [P, NT])
        xh = sb("ln_out", [P, NT * C])
        xh3 = sb("ln3_tokens", [P, NT * B * C])
        xh3T = sb("ln3_channels", [P, 2 * N])
        t2T = sb("tokens_channels", [P, 2 * N])
        wx = sb("wx", [P, 2 * N])
        wx16 = sb("wx_fp16", [P, 2 * N], f16)
        v16 = sb("v_fp16", [P, P], f16)
        y16 = [sb(f"y_fp16_{i}", [P, 2, N + 1], f16) for i in range(2)]
        y32 = [sb(f"y_{i}", [P, 2, N + 1]) for i in range(2)]
        zsw = sb("pre_activation", [P, 4, CW])
        bst = sb("bn_stats", [P, 4, 6])
        bmv = sb("bn_mean_var", [P, 2])
        bmc = sb("bn_mean", [P, 2])
        bwk = sb("bn_scratch", [P, 8])
        dmax = sb("last_step_max", [P, 2])
        flag = sb("not_solved", [1, 2], i32)
        zseq = sb("seq_pre_activation", [P, 2])
        diff = zsw[:].rearrange("p k c -> p (k c)")
        outt = xh3T

        banks = [ctx.enter_context(nc.psum_tensor(f"bank{i}", [P, CW], f32)) for i in range(8)]
        ST, MX, ZT, PJ = banks[0:3], banks[3:5], banks[5:7], banks[7]

        cs, as_ = Sems(sem, "conv"), Sems(sem, "attn")
        s_x = sem("x_loaded")
        s_cw = sem("conv_weights_loaded")
        s_tok = sem("tokens_loaded")
        s_w = sem("attn_weights_loaded")
        s_cst = sem("constants_loaded")
        s_ffn = sem("ffn_loaded")
        s_init = sem("dve_constants_ready")
        s_pinit = sem("pool_constants_ready")
        s_wt = sem("transposed_weights_in_psum")
        s_wtc = sem("transposed_weights_copied")
        s_am = sem("qk_and_projection_matrices_in_psum")
        s_ahi = sem("qk_matrix_high_ready")
        s_amd = sem("attn_matrices_ready")
        s_chain = sem("dve_chain")
        s_xt = sem("ln_values_ready")
        s_xtp = sem("ln_keys_in_psum")
        s_xs = sem("ln_keys_ready")
        s_l3 = sem("ln3_ready")
        s_tr = sem("final_transposes_in_psum")
        s_trc = sem("final_transposes_copied")
        s_trd = sem("residual_transposes_copied")
        s_wxp = sem("wx_in_psum")
        s_bn1 = sem("bn_means_local")
        s_bn2 = sem("bn_mean_in_psum")
        s_bn3 = sem("bn_var_local")
        s_bn4 = sem("bn_var_in_psum")
        s_bn5 = sem("bn_affine_ready")
        s_wx = sem("wx_ready")
        s_wx16 = sem("wx16_ready")
        s_v = sem("sweep_products")
        s_z = sem("sweep_pre_activations")
        s_y = sem("sweep_chunks")
        s_dm = sem("last_step_max_ready")
        s_dmt = sem("last_step_max_transposed")
        s_flag = sem("flag_ready")
        s_sv = sem("sequential_products")
        s_sz = sem("sequential_pre_activations")
        s_sy = sem("sequential_steps")
        s_out = sem("out_added")
        s_store = sem("out_stored")

        block = ctx.enter_context(nc.Block())
        CHAIN = [0]

        def by_head(t, r):
            return t[:].rearrange("p (g r c) -> p g r c", r=2, c=P)[:, :, r, :]

        def link(ins):
            CHAIN[0] += 1
            ins.then_inc(s_chain, 1)
            nc.vector.wait_ge(s_chain, CHAIN[0])


        def pe_prep_wait(ph, s, u, k):
            g = u * ph.nprep + k
            if not isinstance(g, int) or g >= MX_RING:
                nc.tensor.wait_ge(s.prep_used, g - MX_RING + 1)

        def pe_bank(ph, par, k):
            return MX[(par * ph.nprep + k) % MX_RING]

        def pe_queries(ph, s, u, par, b, h, k):
            pe_prep_wait(ph, s, u, k)
            o = pe_bank(ph, par, k)
            r = xs[:, ds(b * N + k * CW, CW)]
            nc.tensor.matmul(o[:], a_hi[:, ds(h * P, P)], r, start=True, stop=False)
            nc.tensor.matmul(o[:], a_lo[:, ds(h * P, P)], r, start=False, stop=True).then_inc(s.prep, 1)

        def pe_conv_prep(ph, s, u, par, k):
            pe_prep_wait(ph, s, u, k)
            o = pe_bank(ph, par, k)
            if k < 4:
                w = cw[:, (k // 2) * P:(k // 2 + 1) * P]
                nc.tensor.matmul(o[:], w, xc[:, u * N + (k % 2) * CW:u * N + (k % 2 + 1) * CW],
                                 start=True, stop=True).then_inc(s.prep, 1)
            else:
                for t in range(TPC):
                    g = u * N + ((k - 4) * TPC + t) * P
                    last = nc.tensor.matmul(o[:, t * P:(t + 1) * P], xc[:, g:g + P], cw[:, 2 * P:3 * P],
                                            start=True, stop=True)
                last.then_inc(s.prep, 1)

        def pe_rowmax(ph, s, u, par, keys, b, i):
            t, part, k0, w, diag = ph.maxes[i]
            pe_prep_wait(ph, s, u, ph.prep + i)
            o = pe_bank(ph, par, ph.prep + i)
            if ph.causal:
                nc.tensor.wait_ge(s.cast, u * NC + t // TPC + 1)
            else:
                nc.tensor.wait_ge(s.prep_used, u * ph.nprep + 4)
            ins = nc.tensor.matmul(o[:, 0:w], q_hi[par][:, t * P:(t + 1) * P], keys[:, ds(b * N + k0, w)],
                                   start=True, stop=not diag)
            if diag:
                ins = nc.tensor.matmul(o[:, w - P:w], identbf[:], masks[:, 1, :], start=False, stop=True)
            ins.then_inc(s.prep, 1)

        def pe_max_transpose(ph, s, u, par):
            k = ph.nprep - 1
            pe_prep_wait(ph, s, u, k)
            nc.tensor.wait_ge(s.rowmax, u + 1)
            nc.tensor.transpose(pe_bank(ph, par, k)[0:NT, 0:P], m8[par][:], cst[:, K_IDENT:K_IDENT + P]) \
                .then_inc(s.prep, 1)

        def pe_scores(ph, s, u, par, keys, b, n, first_unit):
            c, j, off, diag = ph.items[n]
            g = u * ph.n + n
            if not (first_unit and n < ST_RING):
                nc.tensor.wait_ge(s.probs, g - ST_RING + 1)
            if n == 0:
                nc.tensor.wait_ge(s.maxrow, 16 * (u + 1))
                nc.tensor.wait_ge(s.prep_used, (u + 1) * ph.nprep)
            o = ST[n % ST_RING] if ph.n % ST_RING == 0 else ST[(par_base(ph, u) + n) % ST_RING]
            lhs = keys[:, ds(b * N + j * P, P)]
            lo, hi = c * CW + off, (c + 1) * CW
            nc.tensor.matmul(o[:, off:CW], lhs, q_hi[par][:, lo:hi], start=True, stop=False)
            ins = nc.tensor.matmul(o[:, off:CW], lhs, q_lo[par][:, lo:hi], start=False, stop=not diag)
            if diag:
                ins = nc.tensor.matmul(o[:, off:off + P], identbf[:], masks[:, 0, :], start=False, stop=True)
            ins.then_inc(s.scores, 1)

        def par_base(ph, u):
            return u * ph.n if isinstance(u, int) else 0

        def slot(ph, u, n, ring):
            return n % ring if ph.n % ring == 0 else (par_base(ph, u) + n) % ring

        def pe_values(ph, s, u, values, b, n, first_unit):
            c, j, off, _ = ph.items[n]
            if n == ph.first[c] and not first_unit:
                nc.tensor.wait_ge(s.zcopied, u * NC + c - 1)
            nc.tensor.wait_ge(s.probs, u * ph.n + n + 1)
            rs, rv = ph.rest_wait(s, u, n)
            nc.tensor.wait_ge(rs, rv)
            q = slot(ph, u, n, P_RING)
            lhs = values[:, ds((b * NT + j) * P, P)]
            nc.tensor.matmul(ZT[c][:, off:CW], lhs, p_hi[:, q, off:CW], start=(n == ph.first[c]), stop=False)
            nc.tensor.matmul(ZT[c][:, off:CW], lhs, p_lo[:, q, off:CW], start=False,
                             stop=(n == ph.last[c])).then_inc(s.values, 1)

        def pe_project(ph, s, u, pr, c, first_unit):
            nc.tensor.wait_ge(s.zcopied, u * NC + c + 1)
            if not (first_unit and c == 0):
                nc.tensor.wait_ge(s.added, u * NC + c)
            for t in range(TPC):
                last = nc.tensor.matmul(PJ[:, t * PO:(t + 1) * PO], zs[:, c, t * P:(t + 1) * P], pr,
                                        start=True, stop=True)
            last.then_inc(s.projected, 1)

        def value_slots(ph):
            return LAG

        def proj_slot(ph, c):
            return ph.last[c] + LAG + 3

        def pe_unit(ph, s, u, par, keys, values, b, pr, prev, nxt, first):
            for n in range(ph.n):
                if nxt is not None and n == 0:
                    nxt(n)
                pe_scores(ph, s, u, par, keys, b, n, first)
                if nxt is not None and n > 0:
                    nxt(n)
                if n >= LAG:
                    pe_values(ph, s, u, values, b, n - LAG, first)
                elif prev is not None:
                    pe_values(ph, s, u - 1, prev[0], prev[1], n - LAG + ph.n, prev[3])
                for c in range(NC):
                    if n == proj_slot(ph, c):
                        pe_project(ph, s, u, pr, c, first)
                    if prev is not None and n == proj_slot(ph, c) - ph.n:
                        pe_project(ph, s, u - 1, prev[2], c, prev[3])

        def pe_drain(ph, s, u, values, b, pr):
            for n in range(ph.n, ph.n + LAG):
                pe_values(ph, s, u, values, b, n - LAG, False)
            pe_project(ph, s, u, pr, NC - 1, False)

        def a_slot_steps(ph, n):
            if ph.causal:
                table = {0: range(0, 2)}
                for i in range(6):
                    table[2 + i] = range(2 + 2 * i, 4 + 2 * i)
                table[9] = range(14, 15)
            else:
                table = {0: range(0, 2), 1: range(2, 4), 2: range(4, 6)}
                for i in range(8):
                    table[3 + i] = range(6 + 2 * i, 8 + 2 * i)
                table[12] = range(22, 23)
            return table.get(n, range(0))

        def pe_a_step(ph, s, u, par, keys, b, h, k):
            if k < ph.prep:
                if ph.causal:
                    if h is not None:
                        pe_queries(ph, s, u, par, b, h, k)
                else:
                    pe_conv_prep(ph, s, u, par, k)
            elif k < ph.nprep - 1:
                pe_rowmax(ph, s, u, par, keys, b, k - ph.prep)
            else:
                pe_max_transpose(ph, s, u, par)

        def pr_of(h):
            return proj[:, ds(h * PO, PO)]

        def pe_attn_unit(u, par, last=False, first=False):
            b, h = u // H, u % H
            v = u + 1
            bn, hn = v // H, v % H
            nxt = None if last else (lambda n: [pe_a_step(ATTN, as_, v, 1 - par, xs, bn, hn, k)
                                                for k in a_slot_steps(ATTN, n)])
            prev = None
            if not first:
                w = u - 1
                prev = (xt, w // H, pr_of(w % H), isinstance(w, int) and w == 0)
            pe_unit(ATTN, as_, u, par, xs, xt, b, pr_of(h), prev, nxt, first)

        def pe_xs_transposes(b):
            pe = nc.tensor
            pe.wait_ge(s_xt, b + 1)
            pe.wait_ge(s_xs, b) if b else None
            if b == 0:
                pe.wait_ge(s_amd, 1)
            o = PT16
            for t in range(NT):
                last = nc.tensor.transpose(o[:, t * P:(t + 1) * P], xt[:, (b * NT + t) * P:(b * NT + t + 1) * P],
                                           ident16[:])
            last.then_inc(s_xtp, 1)

        PT16 = PJ[:].bitcast(f16)

        @block.tensor
        def _(pe):
            pe.wait_ge(s_cst, 16)
            pe.wait_ge(s_w, 64)
            diffm = cst[0:C, K_DIFF:K_DIFF + P]
            for i, w in enumerate((wq, wk, wv)):
                for p in range(H // 2):
                    last = nc.tensor.matmul(banks[i][:, p * P:(p + 1) * P], w[:, p * P:(p + 1) * P], diffm,
                                            start=True, stop=True)
                last.then_inc(s_wt, 1)
            pe.wait_ge(s_wtc, 3)
            for h in range(H):
                r = C * (h % 2)
                o = banks[3 + h % 2][:, (h // 2) * P:(h // 2 + 1) * P]
                nc.tensor.matmul(o, wqT[r:r + C, h // 2, :], wkT[r:r + C, h // 2, :], start=True, stop=True)
            for h in range(H):
                r = C * (h % 2)
                last = nc.tensor.matmul(banks[5 + h % 2][:, (h // 2) * C:(h // 2 + 1) * C], wvT[r:r + C, h // 2, :],
                                        wo[r:r + C, h // 2, :], start=True, stop=True)
            last.then_inc(s_am, 1)

            pe.wait_ge(s_x, 16)
            pe.wait_ge(s_cw, 32)
            pe.wait_ge(s_init, 1)
            pe.wait_ge(s_amd, 1)
            for k in range(CONV.nprep):
                pe_a_step(CONV, cs, 0, 0, cxs, 0, None, k)
            for u in range(B):
                nxt = None if u == B - 1 else (lambda n, v=u + 1: [pe_a_step(CONV, cs, v, v % 2, cxs, v, None, k)
                                                                   for k in a_slot_steps(CONV, n)])
                prev = (cxt, u - 1, cproj[:], u - 1 == 0) if u else None
                pe_unit(CONV, cs, u, u % 2, cxs, cxt, u, cproj[:], prev, nxt, u == 0)
            pe_drain(CONV, cs, B - 1, cxt, B - 1, cproj[:])

            pe.wait_ge(cs.added, B * NC)
            for b in range(B):
                pe_xs_transposes(b)

            pe.wait_ge(s_xs, B)
            for k in range(ATTN.nprep):
                pe_a_step(ATTN, as_, 0, 0, xs, 0, 0, k)
            pe_attn_unit(0, 0, first=True)
            with pe.Fori(0, (UNITS - 2) // 2) as i:
                pe_attn_unit(1 + 2 * i, 1)
                pe_attn_unit(2 + 2 * i, 0)
            pe_attn_unit(UNITS - 1, 1, last=True)
            pe_drain(ATTN, as_, UNITS - 1, xt, B - 1, pr_of(H - 1))

            pe.wait_ge(as_.added, UNITS * NC)
            idt = cst[:, K_IDENT:K_IDENT + P]
            for k in range(4):
                for t in range(TPC):
                    tile = (k % 2) * TPC + t
                    g = tile * B * C + (k // 2) * P
                    last = nc.tensor.transpose(banks[k][:, t * P:(t + 1) * P], tok[:, g:g + P], idt)
                last.then_inc(s_tr, 1)
            pe.wait_ge(s_l3, 1)
            for k in range(4):
                for t in range(TPC):
                    tile = (k % 2) * TPC + t
                    g = tile * B * C + (k // 2) * P
                    last = nc.tensor.transpose(banks[4 + k][:, t * P:(t + 1) * P], xh3[:, g:g + P], idt)
                last.then_inc(s_tr, 1)
            pe.wait_ge(s_ffn, 32)
            for k in range(4):
                pe.wait_ge(s_trc, k + 1)
                pe.wait_ge(s_trd, k + 1)
                nc.tensor.matmul(banks[k][:], ffn_w[:, 0, :], xh3T[:, k * CW:(k + 1) * CW],
                                 start=True, stop=True).then_inc(s_wxp, 1)
            pe.wait_ge(s_bn1, 1)
            nc.tensor.matmul(banks[4][:, 0:1], cst[:, K_AVG:K_AVG + P], bmv[:, 0:1],
                             start=True, stop=True).then_inc(s_bn2, 1)
            pe.wait_ge(s_bn3, 1)
            nc.tensor.matmul(banks[5][:, 0:1], cst[:, K_AVG:K_AVG + P], bwk[:, 2:3],
                             start=True, stop=True).then_inc(s_bn4, 1)

            pe.wait_ge(s_wx16, 1)
            for w in range(HALF_SWEEPS):
                for k in range(4):
                    pe.wait_ge(s_y, 4 * w + k + 1)
                    yp = y16[w % 2][:, k // 2, (k % 2) * CW:(k % 2) * CW + CW]
                    nc.tensor.matmul(banks[k][:], ident16[:], wx16[:, k * CW:(k + 1) * CW], start=True, stop=False)
                    nc.tensor.matmul(banks[k][:], v16[:], yp, start=False, stop=True).then_inc(s_v, 1)
            for w in range(FULL_SWEEPS):
                for k in range(4):
                    pe.wait_ge(s_y, 4 * (HALF_SWEEPS + w) + k + 1)
                    yp = y32[w % 2][:, k // 2, (k % 2) * CW:(k % 2) * CW + CW]
                    nc.tensor.matmul(banks[k][:], ffn_w[:, 1, :], yp, start=True, stop=True).then_inc(s_v, 1)
            pe.wait_ge(s_dm, 1)
            nc.tensor.transpose(banks[4][0:1, 0:P], dmax[:, 0:1], cst[:, K_IDENT:K_IDENT + P]).then_inc(s_dmt, 1)
            pe.wait_ge(s_flag, 1)
            f = pe.value_load(flag[0:1, 0:1], min_val=0, max_val=1)
            yl = y32[FULL_SWEEPS % 2]
            with pe.If(f > 0):
                with pe.Fori(0, N) as t:
                    pe.wait_ge(s_sy, t + 1)
                    nc.tensor.matmul(banks[6][:, 0:2], ffn_w[:, 1, :], yl[:, :, ds(t, 1)].rearrange("p a b -> p (a b)"),
                                     start=True, stop=True).then_inc(s_sv, 1)

        def act_item(ph, s, u, n, first_unit, scale):
            c, j, off, _ = ph.items[n]
            g = u * ph.n + n
            nc.scalar.wait_ge(s.scores, g + 1)
            if not (first_unit and n < E_RING):
                rs, rv = ph.rest_wait(s, *ph.back(u, n, E_RING))
                nc.scalar.wait_ge(rs, rv)
            if not (first_unit and n < P_RING):
                nc.scalar.wait_ge(s.values, g - P_RING + 1)
            o = ST[slot(ph, u, n, ST_RING)]
            e, q = slot(ph, u, n, E_RING), slot(ph, u, n, P_RING)
            nc.scalar.activation(e32[:, e, off:CW], o[:, off:CW], ACT.Exp, scale=scale).then_inc(s.probs32, 1)
            nc.scalar.activation(p_hi[:, q, off:CW], o[:, off:CW], ACT.Exp, scale=scale).then_inc(s.probs, 1)

        def act_cast(ph, s, u, par, k):
            nc.scalar.wait_ge(s.prep, u * ph.nprep + k + 1)
            src = MX[(par * ph.nprep + k) % MX_RING]
            if ph.causal:
                dst = q_hi[par][:, k * CW:(k + 1) * CW]
            elif k < 2:
                dst = cxs[:, u * N + k * CW:u * N + (k + 1) * CW]
            elif k < 4:
                dst = q_hi[par][:, (k - 2) * CW:(k - 1) * CW]
            else:
                dst = cxt[:, (u * NT + (k - 4) * TPC) * P:(u * NT + (k - 3) * TPC) * P]
            nc.scalar.activation(dst, src[:], ACT.Copy).then_inc(s.cast, 1)

        def act_zcopy(ph, s, u, c, first_unit):
            nc.scalar.wait_ge(s.values, u * ph.n + ph.last[c] + 1)
            nc.scalar.activation(zs[:, c, :], ZT[c][:], ACT.Copy).then_inc(s.zcopied, 1)

        def zslot(ph, c):
            return ph.last[c] + LAG - 1

        def act_unit(ph, s, u, par, first, prev_first, has_prev, nxt, scale):
            for n in range(ph.n):
                if nxt:
                    for k in a_slot_steps(ph, n):
                        if k < ph.prep:
                            act_cast(ph, s, u + 1, 1 - par, k)
                act_item(ph, s, u, n, first, scale)
                for c in range(NC):
                    if n == zslot(ph, c):
                        act_zcopy(ph, s, u, c, first)
                    if has_prev and n == zslot(ph, c) - ph.n:
                        act_zcopy(ph, s, u - 1, c, prev_first)

        @block.scalar
        def _(act):
            act.dma_start(xc[:].rearrange("c (b n) -> c b n", b=B), x_cm.rearrange("b c n -> c b n")).then_inc(s_x, 16)
            for i, (t, src) in enumerate(((wq, w_q), (wk, w_k), (wv, w_v))):
                act.dma_start(t[:], src).then_inc(s_w, 16)
            act.dma_start(wo[:], w_o.rearrange("(g p) c -> p g c", p=P)).then_inc(s_w, 16)
            act.wait_ge(s_wt, 3)
            for t, bk in ((wqT, 0), (wkT, 1), (wvT, 2)):
                nc.scalar.activation(t[:].rearrange("p g c -> p (g c)"), banks[bk][:], ACT.Copy).then_inc(s_wtc, 1)
            act.wait_ge(s_am, 1)
            for r in range(2):
                nc.scalar.activation(by_head(a_hi, r), banks[3 + r][:].rearrange("p (g c) -> p g c", c=P), ACT.Copy)
                ins = nc.scalar.activation(proj[:].rearrange("p (g r c) -> p g r c", r=2, c=PO)[:, :, r, 0:C],
                                           banks[5 + r][:, 0:H // 2 * C].rearrange("p (g c) -> p g c", c=C), ACT.Copy)
            ins.then_inc(s_ahi, 1)
            for k in range(CONV.prep):
                act_cast(CONV, cs, 0, 0, k)
            for u in range(B):
                act_unit(CONV, cs, u, u % 2, u == 0, u == 1, u > 0, u < B - 1, 1.0)
            act_zcopy(CONV, cs, B - 1, NC - 1, False)
            for b in range(B):
                act.wait_ge(s_xtp, b + 1)
                nc.scalar.activation(xs[:, b * N:(b + 1) * N], PT16, ACT.Copy).then_inc(s_xs, 1)
            for k in range(ATTN.prep):
                act_cast(ATTN, as_, 0, 0, k)
            act_unit(ATTN, as_, 0, 0, True, False, False, True, SCALE)
            with act.Fori(0, (UNITS - 2) // 2) as i:
                act_unit(ATTN, as_, 1 + 2 * i, 1, False, True, True, True, SCALE)
                act_unit(ATTN, as_, 2 + 2 * i, 0, False, False, True, True, SCALE)
            act_unit(ATTN, as_, UNITS - 1, 1, False, False, True, False, SCALE)
            act_zcopy(ATTN, as_, UNITS - 1, NC - 1, False)
            for k in range(4):
                act.wait_ge(s_tr, 5 + k)
                nc.scalar.activation(xh3T[:, k * CW:(k + 1) * CW], banks[4 + k][:], ACT.Copy).then_inc(s_trc, 1)
            act.wait_ge(s_bn5, 1)
            act.wait_ge(s_wxp, 4)
            for k in range(4):
                nc.scalar.activation(wx[:, k * CW:(k + 1) * CW], banks[k][:], ACT.Identity,
                                     scale=bwk[:, 5:6], bias=bwk[:, 6:7]).then_inc(s_wx, 1)
            act.wait_ge(s_wx, 4)
            for k in range(4):
                nc.scalar.activation(y16[0][:, k // 2, 1 + (k % 2) * CW:1 + (k % 2) * CW + CW],
                                     wx[:, k * CW:(k + 1) * CW], ACT.Sigmoid).then_inc(s_y, 1)
            for w in range(HALF_SWEEPS):
                dst = y16[(w + 1) % 2] if w < HALF_SWEEPS - 1 else y32[0]
                for k in range(4):
                    act.wait_ge(s_v, 4 * w + k + 1)
                    if w >= 1:
                        act.wait_ge(s_v, min(4 * w + k + 1, 4 * (w - 1) + k + 2))
                    nc.scalar.activation(dst[:, k // 2, 1 + (k % 2) * CW:1 + (k % 2) * CW + CW],
                                         banks[k][:], ACT.Sigmoid).then_inc(s_y, 1)
            for w in range(FULL_SWEEPS):
                dst = y32[(w + 1) % 2]
                for k in range(4):
                    act.wait_ge(s_z, 4 * w + k + 1)
                    nc.scalar.activation(dst[:, k // 2, 1 + (k % 2) * CW:1 + (k % 2) * CW + CW],
                                         zsw[:, k, :], ACT.Sigmoid).then_inc(s_y, 1)
            act.wait_ge(s_flag, 1)
            f = act.value_load(flag[0:1, 0:1], min_val=0, max_val=1)
            yl = y32[FULL_SWEEPS % 2]
            with act.If(f > 0):
                with act.Fori(0, N) as t:
                    act.wait_ge(s_sz, t + 1)
                    nc.scalar.activation(yl[:, :, ds(t + 1, 1)].rearrange("p a b -> p (a b)"), zseq[:],
                                         ACT.Sigmoid).then_inc(s_sy, 1)

        def rest_item(eng, ph, s, u, n, first_unit):
            off = ph.items[n][2]
            g = u * ph.n + n
            eng.wait_ge(s.probs, g + 1)
            if not (first_unit and n < P_RING):
                eng.wait_ge(s.values, g - P_RING + 1)
            e, q = slot(ph, u, n, E_RING), slot(ph, u, n, P_RING)
            rs, _ = ph.rest_wait(s, u, n)
            eng.tensor_tensor(out=p_lo[:, q, off:CW], in0=e32[:, e, off:CW], in1=p_hi[:, q, off:CW],
                              op=ALU.subtract).then_inc(rs, 1)

        def dve_a_step(ph, s, u, par, k):
            dve = nc.vector
            src = MX[(par * ph.nprep + k) % MX_RING]
            dve.wait_ge(s.prep, u * ph.nprep + k + 1)
            mxs = (amx if ph.causal else cmx)[par]
            if k < ph.prep:
                dve.wait_ge(s.cast, u * ph.prep + k + 1)
                if ph.causal:
                    a = q_hi[par][:, k * CW:(k + 1) * CW]
                    nc.vector.tensor_tensor(out=q_lo[par][:, k * CW:(k + 1) * CW], in0=src[:], in1=a,
                                            op=ALU.subtract).then_inc(s.prep_used, 1)
                elif k < 2:
                    a = cxs[64:96, u * N + k * CW:u * N + (k + 1) * CW]
                    nc.vector.memset(cxs[0:1, u * N + k * CW:u * N + (k + 1) * CW], 1.0)
                    nc.vector.tensor_tensor(out=a, in0=src[64:96, :], in1=a, op=ALU.subtract).then_inc(s.prep_used, 1)
                elif k < 4:
                    a = q_hi[par][:, (k - 2) * CW:(k - 1) * CW]
                    nc.vector.tensor_tensor(out=q_lo[par][:, (k - 2) * CW:(k - 1) * CW], in0=src[:], in1=a,
                                            op=ALU.subtract).then_inc(s.prep_used, 1)
                else:
                    g = (u * NT + (k - 4) * TPC) * P
                    a = cxt[:, g:g + CW].rearrange("p (t c) -> p t c", t=TPC)
                    nc.vector.memset(a[:, :, 0:1], 1.0)
                    nc.vector.tensor_tensor(out=a[:, :, 64:96], in0=src[:].rearrange("p (t c) -> p t c", t=TPC)[:, :, 64:96],
                                            in1=a[:, :, 64:96], op=ALU.subtract).then_inc(s.prep_used, 1)
            elif k < ph.nprep - 1:
                t, part, k0, w, diag = ph.maxes[k - ph.prep]
                nc.vector.reduce_max(mxs[:, t, part:part + 1], src[:, 0:w], AX).then_inc(s.prep_used, 1)
            else:
                nc.vector.tensor_scalar(mrow[par][:], src[0:NT, 0:P], -1.0, None, ALU.mult).then_inc(s.prep_used, 1)

        def dve_rowmax(ph, s, u, par):
            mxs = (amx if ph.causal else cmx)[par]
            nc.vector.wait_ge(s.prep_used, (u + 1) * ph.nprep - 1)
            nc.vector.reduce_max(m8[par][:], mxs[:], AX).then_inc(s.rowmax, 1)

        def dve_add(ph, s, u, b, c, first_unit):
            dve = nc.vector
            dve.wait_ge(s.projected, u * NC + c + 1)
            if not (first_unit and c == 0):
                dve.wait_ge(s.added, u * NC + c)
            pj = PJ[:, 0:TPC * PO].rearrange("p (t c) -> p t c", c=PO)
            nc.vector.reciprocal(rden[:, c, :], pj[:, :, C:PO].rearrange("p t c -> p (t c)")).then_inc(s.recip, 1)
            dve.wait_ge(s.recip, u * NC + c + 1)
            for t in range(TPC):
                dst = tok[:, ds(b * C + (c * TPC + t) * B * C, C)]
                last = nc.vector.scalar_tensor_tensor(out=dst, in0=pj[:, t, 0:C], scalar=rden[:, c, t:t + 1],
                                                      in1=dst, op0=ALU.mult, op1=ALU.add)
            last.then_inc(s.added, 1)

        def dve_drain(ph, s, u, b):
            for n in range(ph.n - REST_LAG, ph.n):
                if n in ph.dve_items:
                    rest_item(nc.vector, ph, s, u, n, False)
            dve_add(ph, s, u, b, NC - 1, False)

        def rowmax_slot(ph):
            return 8 if ph.causal else 11

        def add_slot(ph, c):
            return ph.last[c] + LAG + 3

        def dve_unit(ph, s, u, par, b, bprev, first, prev_first, has_prev, nxt):
            for n in range(ph.n):
                if nxt:
                    for k in a_slot_steps(ph, n):
                        dve_a_step(ph, s, u + 1, 1 - par, k)
                    if n == rowmax_slot(ph):
                        dve_rowmax(ph, s, u + 1, 1 - par)
                if n - REST_LAG in ph.dve_items:
                    rest_item(nc.vector, ph, s, u, n - REST_LAG, first)
                if has_prev and n - REST_LAG + ph.n in ph.dve_items:
                    rest_item(nc.vector, ph, s, u - 1, n - REST_LAG + ph.n, prev_first)
                for c in range(NC):
                    if n == add_slot(ph, c):
                        dve_add(ph, s, u, b, c, first)
                    if has_prev and n == add_slot(ph, c) - ph.n:
                        dve_add(ph, s, u - 1, bprev, c, prev_first)

        def dve_rsqrt(r, v, w, n):
            link(nc.vector.tensor_scalar(r.bitcast(i32), v.bitcast(i32), -0.5, 1597463007.0, ALU.mult, ALU.add))
            for _ in range(4):
                link(nc.vector.tensor_tensor(out=w, in0=r, in1=r, op=ALU.mult))
                link(nc.vector.tensor_tensor(out=w, in0=w, in1=v, op=ALU.mult))
                link(nc.vector.tensor_scalar(w, w, -0.5, 1.5, ALU.mult, ALU.add))
                link(nc.vector.tensor_tensor(out=r, in0=r, in1=w, op=ALU.mult))

        def dve_layernorm(b, dst, eps):
            for t in range(NT):
                g = (t * B + b) * C
                ins = nc.vector.bn_stats(stats[:, t, :], tok[:, g:g + C])
            link(ins)
            for t in range(NT):
                ins = nc.vector.bn_aggr(mv[:, t, :], stats[:, t, :])
            link(ins)
            link(nc.vector.tensor_scalar_add(nwt2[:], mv[:, :, 1:2].rearrange("p t c -> p (t c)"), eps))
            dve_rsqrt(rstd[:], nwt2[:], nwt[:], NT)
            for t in range(NT):
                g = (t * B + b) * C
                ins = nc.vector.tensor_scalar(dst(t), tok[:, g:g + C], mv[:, t, 0:1], rstd[:, t:t + 1],
                                              ALU.subtract, ALU.mult)
            link(ins)

        nwt2 = sb("ln_var_eps", [P, NT])

        @block.vector
        def _(dve):
            dve.wait_ge(s_cst, 16)
            nc.vector.tensor_copy(ident16[:], cst[:, K_IDENT:K_IDENT + P])
            nc.vector.tensor_copy(identbf[:], cst[:, K_IDENT:K_IDENT + P])
            nc.vector.tensor_copy(masks[:].rearrange("p a c -> p (a c)"), cst[:, K_MASK_T:K_MASK_T + 2 * P]) \
                .then_inc(s_init, 1)
            for i in range(2):
                nc.vector.memset(amx[i][:], -3e38)
                nc.vector.memset(y16[i][:, :, 0:1], 0.0)
                nc.vector.memset(y32[i][:, :, 0:1], 0.0)
            pj3 = proj[:].rearrange("p (h c) -> p h c", c=PO)
            link(nc.vector.memset(pj3[:, :, C:PO], 0.0))
            link(nc.vector.memset(pj3[0:1, :, C:PO], 1.0))
            dve.wait_ge(s_ahi, 1)
            for r in range(2):
                ins = nc.vector.tensor_tensor(out=by_head(a_lo, r), in0=banks[3 + r][:].rearrange("p (g c) -> p g c", c=P),
                                              in1=by_head(a_hi, r), op=ALU.subtract)
            ins.then_inc(s_amd, 1)
            dve.wait_ge(s_tok, 16)
            for k in range(CONV.nprep):
                if k == CONV.nprep - 1:
                    dve_rowmax(CONV, cs, 0, 0)
                dve_a_step(CONV, cs, 0, 0, k)
            for u in range(B):
                dve_unit(CONV, cs, u, u % 2, u, u - 1, u == 0, u == 1, u > 0, u < B - 1)
            dve_drain(CONV, cs, B - 1, B - 1)
            dve.wait_ge(cs.added, B * NC)
            for b in range(B):
                dve_layernorm(b, lambda t: xh[:, t * C:(t + 1) * C], 1e-5)
                x3 = xh[:].rearrange("p (t c) -> p t c", c=C)
                v3 = xt[:, b * NT * P:(b + 1) * NT * P].rearrange("p (t c) -> p t c", c=P)
                link(nc.vector.tensor_copy(v3[:, :, 0:C], x3))
                link(nc.vector.tensor_tensor(out=v3[:, :, C:P], in0=x3, in1=v3[:, :, 0:C], op=ALU.subtract))
                nc.vector.memset(v3[:, :, 0:1], 1.0)
                nc.vector.memset(v3[:, :, C:C + 1], 0.0).then_inc(s_xt, 1)
            for k in range(ATTN.nprep):
                if k == ATTN.nprep - 1:
                    dve_rowmax(ATTN, as_, 0, 0)
                dve_a_step(ATTN, as_, 0, 0, k)
            dve_unit(ATTN, as_, 0, 0, 0, 0, True, False, False, True)
            with dve.Fori(0, (UNITS - 2) // 2) as i:
                dve_unit(ATTN, as_, 1 + 2 * i, 1, (1 + 2 * i) // H, (2 * i) // H, False, True, True, True)
                dve_unit(ATTN, as_, 2 + 2 * i, 0, (2 + 2 * i) // H, (1 + 2 * i) // H, False, False, True, True)
            dve_unit(ATTN, as_, UNITS - 1, 1, B - 1, B - 1, False, False, True, False)
            dve_drain(ATTN, as_, UNITS - 1, B - 1)
            dve.wait_ge(as_.added, UNITS * NC)
            for b in range(B):
                dve_layernorm(b, lambda t: xh3[:, (t * B + b) * C:(t * B + b + 1) * C], 1e-5)
            dve.wait_ge(s_ffn, 32)
            nc.vector.tensor_copy(v16[:], ffn_w[:, 1, :]).then_inc(s_l3, 1)
            for k in range(4):
                dve.wait_ge(s_tr, k + 1)
                nc.vector.tensor_copy(t2T[:, k * CW:(k + 1) * CW], banks[k][:]).then_inc(s_trd, 1)
            for k in range(4):
                dve.wait_ge(s_wxp, k + 1)
                ins = nc.vector.bn_stats(bst[:, k, :], banks[k][:])
            link(ins)
            nc.vector.bn_aggr(bmv[:], bst[:].rearrange("p k c -> p (k c)")).then_inc(s_bn1, 1)
            dve.wait_ge(s_bn1, 1)
            dve.wait_ge(s_bn2, 1)
            link(nc.vector.tensor_copy(bwk[:, 0:1], banks[4][:, 0:1]))
            link(nc.vector.tensor_tensor(out=bwk[:, 1:2], in0=bmv[:, 0:1], in1=bwk[:, 0:1], op=ALU.subtract))
            link(nc.vector.tensor_tensor(out=bwk[:, 1:2], in0=bwk[:, 1:2], in1=bwk[:, 1:2], op=ALU.mult))
            nc.vector.tensor_tensor(out=bwk[:, 2:3], in0=bwk[:, 1:2], in1=bmv[:, 1:2], op=ALU.add).then_inc(s_bn3, 1)
            dve.wait_ge(s_bn4, 1)
            link(nc.vector.tensor_scalar_add(bwk[:, 3:4], banks[5][:, 0:1], 1e-5))
            dve_rsqrt(bwk[:, 4:5], bwk[:, 3:4], bwk[:, 7:8], 1)
            dve.wait_ge(s_ffn, 32)
            link(nc.vector.tensor_tensor(out=bwk[:, 5:6], in0=bwk[:, 4:5], in1=gbt[:, 0:1], op=ALU.mult))
            link(nc.vector.tensor_tensor(out=bwk[:, 7:8], in0=bwk[:, 5:6], in1=bwk[:, 0:1], op=ALU.mult))
            nc.vector.tensor_tensor(out=bwk[:, 6:7], in0=gbt[:, 1:2], in1=bwk[:, 7:8],
                                    op=ALU.subtract).then_inc(s_bn5, 1)
            dve.wait_ge(s_wx, 4)
            nc.vector.tensor_copy(wx16[:], wx[:]).then_inc(s_wx16, 1)
            for w in range(FULL_SWEEPS):
                for k in range(4):
                    dve.wait_ge(s_v, 4 * (HALF_SWEEPS + w) + k + 1)
                    if w:
                        dve.wait_ge(s_y, 4 * (HALF_SWEEPS + w) + k + 1)
                    nc.vector.tensor_tensor(out=zsw[:, k, :], in0=banks[k][:], in1=wx[:, k * CW:(k + 1) * CW],
                                            op=ALU.add).then_inc(s_z, 1)
            ya, yb = y32[(FULL_SWEEPS - 1) % 2], y32[FULL_SWEEPS % 2]
            dve.wait_ge(s_y, 4 * (1 + HALF_SWEEPS + FULL_SWEEPS))
            link(nc.vector.tensor_tensor(out=diff.rearrange("p (a n) -> p a n", a=2), in0=ya[:, :, 1:N + 1],
                                         in1=yb[:, :, 1:N + 1], op=ALU.subtract))
            nc.vector.tensor_reduce(out=dmax[:, 0:1], in_=diff, axis=AX, op=ALU.max,
                                    apply_absolute_value=True).then_inc(s_dm, 1)
            dve.wait_ge(s_dmt, 1)
            link(nc.vector.reduce_max(dmax[0:1, 1:2], banks[4][0:1, 0:P], AX))
            nc.vector.tensor_scalar(flag[0:1, 0:1], dmax[0:1, 1:2], RESIDUAL_LIMIT, None, ALU.is_gt).then_inc(s_flag, 1)
            dve.wait_ge(s_flag, 1)
            f = dve.value_load(flag[0:1, 0:1], min_val=0, max_val=1)
            with dve.If(f > 0):
                nc.vector.memset(diff[:, 0:1], 0.0).then_inc(s_sy, 1)
                wx2 = wx[:].rearrange("p (a n) -> p a n", a=2)
                with dve.Fori(0, N) as t:
                    dve.wait_ge(s_sv, t + 1)
                    nc.vector.tensor_tensor(out=zseq[:], in0=banks[6][:, 0:2],
                                            in1=wx2[:, :, ds(t, 1)].rearrange("p a b -> p (a b)"),
                                            op=ALU.add).then_inc(s_sz, 1)
                dve.wait_ge(s_sy, N + 1)
            link(nc.vector.memset(diff[:, 0:1], 0.0))
            for a in range(2):
                nc.vector.tensor_tensor(out=outt[:, a * N:(a + 1) * N], in0=t2T[:, a * N:(a + 1) * N],
                                        in1=yb[:, a, 1:N + 1], op=ALU.add).then_inc(s_out, 1)

        def pool_unit(ph, s, u, first):
            for n in ph.pool_items:
                rest_item(nc.gpsimd, ph, s, u, n, first)

        @block.gpsimd
        def _(pool):
            for u in range(B):
                pool_unit(CONV, cs, u, u == 0)
            pool_unit(ATTN, as_, 0, True)
            with pool.Fori(0, (UNITS - 2) // 2) as i:
                pool_unit(ATTN, as_, 1 + 2 * i, False)
                pool_unit(ATTN, as_, 2 + 2 * i, False)
            pool_unit(ATTN, as_, UNITS - 1, False)

        def sp_maxrow(ph, s, u, par):
            nc.sync.wait_ge(s.prep_used, (u + 1) * ph.nprep)
            nc.sync.dma_start(q_hi[par][0:1, :], mrow[par][:]).then_inc(s.maxrow, 16)

        @block.sync
        def _(sp):
            sp.dma_start(cst[:], const).then_inc(s_cst, 16)
            sp.dma_start(cw[:], conv_w).then_inc(s_cw, 16)
            sp.dma_start(cproj[:], conv_proj).then_inc(s_cw, 16)
            for t in range(NT):
                pass
            sp.dma_start(tok[:].rearrange("p (t b c) -> p t b c", t=NT, b=B)[:, :, :, :].rearrange("p t b c -> p (t b c)"),
                         x_tm).then_inc(s_tok, 16)
            sp.dma_start(ffn_w[:], ffn).then_inc(s_ffn, 16)
            sp.dma_start(gbt[:], gb).then_inc(s_ffn, 16)
            for u in range(B):
                sp_maxrow(CONV, cs, u, u % 2)
            sp_maxrow(ATTN, as_, 0, 0)
            with sp.Fori(0, (UNITS - 2) // 2) as i:
                sp_maxrow(ATTN, as_, 1 + 2 * i, 1)
                sp_maxrow(ATTN, as_, 2 + 2 * i, 0)
            sp_maxrow(ATTN, as_, UNITS - 1, 1)
            for a in range(2):
                sp.wait_ge(s_out, a + 1)
                sp.dma_start(out[a * P:(a + 1) * P, :], outt[:, a * N:(a + 1) * N]).then_inc(s_store, 16)
            sp.wait_ge(s_store, 32)


def kernel(x, L0_conv_wq, L0_conv_wk, L0_conv_wv, L0_conv_wo, L1_attn_Wq, L1_attn_Wk, L1_attn_Wv, L1_attn_Wo,
           L1_ffn_W, L1_ffn_V, L1_ffn_gamma, L1_ffn_beta):
    import numpy as np
    import concourse.bacc as bacc
    from concourse.bass_utils import run_bass_kernel_spmd as run

    x = np.asarray(x)
    f = x.dtype
    x_cm = np.ascontiguousarray(x.reshape(B, C, N))
    x_tm = np.ascontiguousarray(x_cm.reshape(B, C, NT, P).transpose(3, 2, 0, 1).reshape(P, NT * B * C))
    conv_w = np.zeros((C, 3, P), f)
    for i, w in enumerate((L0_conv_wq, L0_conv_wk, L0_conv_wv)):
        conv_w[:, i, MC:2 * MC] = conv_w[:, i, 2 * MC:3 * MC] = np.asarray(w).T
    conv_proj = np.zeros((P, PO), f)
    conv_proj[MC:2 * MC, 0:C] = conv_proj[2 * MC:3 * MC, 0:C] = np.asarray(L0_conv_wo).T
    conv_proj[0, C] = 1.0
    ffn = np.zeros((P, 2, P), f)
    for i, w in enumerate((L1_ffn_W, L1_ffn_V)):
        ffn[0:C, i, 0:C] = ffn[C:P, i, C:P] = np.asarray(w).T
    gb = np.stack([np.tile(np.asarray(L1_ffn_gamma), 2), np.tile(np.asarray(L1_ffn_beta), 2)], axis=1)
    const = np.zeros((P, CONST_COLS), f)
    r, c = np.arange(P)[:, None], np.arange(P)[None, :]
    const[:, K_IDENT:K_IDENT + P] = r == c
    const[:, K_AVG:K_AVG + P] = np.where(r % C == c % C, 0.5, 0.0)
    const[:, K_MASK_T:K_MASK_T + P] = np.where(c < r, NEG, 0.0)
    const[:, K_MASK_R:K_MASK_R + P] = np.where(c > r, NEG, 0.0)
    const[:, K_DIFF:K_DIFF + P] = np.where(c % C == 0, 0.0, np.where(r == c % C, 1.0, np.where(r == 0, -1.0, 0.0)))

    arrays = dict(x_cm=x_cm, x_tm=x_tm, conv_w=conv_w.reshape(C, 3 * P), conv_proj=conv_proj,
                  w_q=np.asarray(L1_attn_Wq), w_k=np.asarray(L1_attn_Wk), w_v=np.asarray(L1_attn_Wv),
                  w_o=np.asarray(L1_attn_Wo), ffn=ffn, gb=gb, const=const)
    arrays = {k: np.ascontiguousarray(v) for k, v in arrays.items()}
    nc = bacc.Bacc("TRN2", target_bir_lowering=False, num_devices=1)
    aps = {k: nc.dram_tensor(f"in_{k}", v.shape, mybir.dt.from_np(v.dtype), kind="ExternalInput").ap()
           for k, v in arrays.items()}
    out = nc.dram_tensor("out", (B * C, N), mybir.dt.float32, kind="ExternalOutput").ap()
    build(nc, out=out, **aps)
    res = run(nc, [{f"in_{k}": v for k, v in arrays.items()}], core_ids=[0])
    return res.results[0]["out"].reshape(x.shape)
```

```python
import concourse.bass as bass
from concourse import mybir
from contextlib import ExitStack

B, C, N = 4, 64, 1024
MC = 32
H, D = 8, 64
P = 128
NT = N // P
CW = 512
NC = N // CW
TPC = CW // P
UNITS = B * H
PO = C + 1

ST_RING, MX_RING, P_RING, E_RING = 3, 2, 12, 6
REST_LAG = 3
KEYS_SLOT, KEYS_SLOT3 = 3, 9
LN1_SLOT = 8
LN3_SLOTS = (9, 10, 11)
LN_EPS = 1e-5
LAST_TR_SLOT, LAST_W_SLOT = 6, 9
LAG = 5

HALF_SWEEPS = 4
FULL_SWEEPS = 7
RESIDUAL_LIMIT = 2.0 ** -21

K_IDENT, K_AVG, K_MASK_T, K_MASK_R, K_DIFF = 0, 128, 256, 384, 512
CONST_COLS = 640
NEG = -1e30


class Sems:

    def __init__(self, sem, tag):
        self.scores = sem(f"{tag}_scores_in_psum")
        self.probs32 = sem(f"{tag}_probs32_written")
        self.probs = sem(f"{tag}_probs_written")
        self.rest_pool = sem(f"{tag}_rest_by_pool")
        self.rest_dve = sem(f"{tag}_rest_by_dve")
        self.values = sem(f"{tag}_values_accumulated")
        self.zcopied = sem(f"{tag}_z_copied")
        self.projected = sem(f"{tag}_chunk_projected")
        self.recip = sem(f"{tag}_recip")
        self.scaled = sem(f"{tag}_chunk_scaled")
        self.added = sem(f"{tag}_chunk_added")
        self.prep = sem(f"{tag}_prep_in_psum")
        self.prep_used = sem(f"{tag}_prep_used")
        self.cast = sem(f"{tag}_high_part_cast")
        self.rowmax = sem(f"{tag}_row_max")
        self.maxrow = sem(f"{tag}_max_row_dma")


class Phase:

    def __init__(self, causal, prep, dve_items):
        self.causal = causal
        self.items = []
        for c in range(NC):
            for j in range(TPC * (c + 1) if causal else NT):
                off = max(0, (j - TPC * c)) * P if causal else 0
                self.items.append((c, j, off, causal and j >= TPC * c))
        self.n = len(self.items)
        self.last = [max(i for i, it in enumerate(self.items) if it[0] == c) for c in range(NC)]
        self.first = [min(i for i, it in enumerate(self.items) if it[0] == c) for c in range(NC)]
        self.maxes = []
        for t in range(NT):
            keys = (t + 1) * P if causal else N
            for part in range((keys + CW - 1) // CW):
                k0 = part * CW
                w = min(CW, keys - k0)
                self.maxes.append((t, part, k0, w, causal and k0 + w == keys))
        self.prep = prep
        self.nprep = prep + len(self.maxes) + 1
        self.dve_items = sorted(dve_items)
        self.pool_items = [i for i in range(self.n) if i not in dve_items]

    def rest_wait(self, s, u, n):
        if n in self.dve_items:
            return s.rest_dve, u * len(self.dve_items) + self.dve_items.index(n) + 1
        return s.rest_pool, u * len(self.pool_items) + self.pool_items.index(n) + 1

    def back(self, u, n, k):
        return (u, n - k) if n >= k else (u - 1, n - k + self.n)


def build(nc, x_cm, x_tm, conv_w, conv_proj, w_q, w_k, w_v, w_o, ffn, gb, const, out):
    f32, f16, bf16, i32 = mybir.dt.float32, mybir.dt.float16, mybir.dt.bfloat16, mybir.dt.int32
    ALU, ACT, AX = mybir.AluOpType, mybir.ActivationFunctionType, mybir.AxisListType.X
    ds = bass.ds

    CONV = Phase(causal=False, prep=6, dve_items={2, 9, 11, 12, 13, 14})
    ATTN = Phase(causal=True, prep=2, dve_items={1, 5, 8})
    SCALE = float(D) ** -0.5

    ctx = ExitStack()
    with ctx:
        def sb(name, shape, dt=f32):
            return ctx.enter_context(nc.sbuf_tensor(name, shape, dt))

        def sem(name):
            return ctx.enter_context(nc.semaphore(name))

        xc = sb("x_channels", [P, B * N])
        x16 = sb("x_split", [P, B * N], f16)
        tok = sb("tokens", [P, NT * B * C])
        cw = sb("conv_weights", [P, 3 * P])
        cw_hi = sb("conv_weights_high", [P, 3 * P], f16)
        cw_lo = sb("conv_weights_low", [P, 3 * P], f16)
        cproj = sb("conv_projection", [P, PO])
        wq = sb("w_q", [C, H * D])
        wk = sb("w_k", [C, H * D])
        wv = sb("w_v", [C, H * D])
        wo = sb("w_o", [P, H // 2, C])
        ffn_w = sb("ffn_weights", [P, 2, P])
        gbt = sb("gamma_beta", [P, 2])
        cst = sb("constants", [P, CONST_COLS])
        ident16 = sb("identity_fp16", [P, P], f16)
        identbf = sb("identity_bf16", [P, P], bf16)
        masks = sb("causal_masks", [P, 2, P], bf16)
        wqT = sb("wq_pairs_T", [P, H // 2, P])
        wkT = sb("wk_pairs_T", [P, H // 2, P])
        wvT = sb("wv_pairs_T", [P, H // 2, P])
        a_hi = sb("qk_matrix_high", [P, H * P], f16)
        a_lo = sb("qk_matrix_low", [P, H * P], f16)
        proj = sb("attn_projection", [P, H * PO])
        cxs = sb("conv_keys", [P, B * N], f16)
        cxt = sb("conv_values", [P, B * NT * P], f16)
        xs = sb("attn_keys", [P, B * N], f16)
        xt = sb("attn_values", [P, B * NT * P], f16)
        q_hi = [sb(f"queries_high{i}", [P, N], f16) for i in range(2)]
        q_lo = [sb(f"queries_low{i}", [P, N], f16) for i in range(2)]
        e32 = sb("probs32", [P, E_RING, CW])
        p_hi = sb("probs_high", [P, P_RING, CW], f16)
        p_lo = sb("probs_low", [P, P_RING, CW], f16)
        zs = sb("z", [P, NC, CW])
        scaled = sb("scaled_chunks", [P, NC, TPC, C])
        rden = sb("reciprocal_denominators", [P, NC, TPC])
        cmx = [sb(f"conv_partial_max{i}", [P, NT, NC]) for i in range(2)]
        amx = [sb(f"attn_partial_max{i}", [P, NT, NC]) for i in range(2)]
        m8 = [sb(f"row_max{i}", [P, NT]) for i in range(2)]
        mrow = [sb(f"minus_max_rows{i}", [NT, P], f16) for i in range(2)]
        stats = sb("ln_stats", [P, NT, 6])
        mv = sb("ln_mean_var", [P, NT * B, 2])
        mv_one = sb("ln_mean_var_of_one_tile", [P, 2])
        rstd = sb("ln_rstd", [P, NT * B])
        var_eps = sb("ln_var_eps", [P, NT * B])
        nwt = sb("newton_scratch", [P, NT * B])
        xh = sb("ln_out", [P, NT * C])
        xh3 = sb("ln3_tokens", [P, NT * B * C])
        xh3T = sb("ln3_channels", [P, 2 * N])
        t2T = sb("tokens_channels", [P, 2 * N])
        wx = xc[:, 2 * N:4 * N]
        wx16 = sb("wx_fp16", [P, 2 * N], f16)
        v16 = sb("v_fp16", [P, P], f16)
        y16 = [sb(f"y_fp16_{i}", [P, 2, N + 1], f16) for i in range(2)]
        y32 = [sb(f"y_{i}", [P, 2, N + 1]) for i in range(2)]
        zsw = xc[:, 0:2 * N].rearrange("p (k c) -> p k c", k=4)
        bst = sb("bn_stats", [P, 4, 6])
        bmv = sb("bn_mean_var", [P, 2])
        bwk = sb("bn_scratch", [P, 8])
        dmax = sb("last_step_max", [P, 6])
        wait_carrier = sb("wait_carrier", [P, 1])
        sig_table = sb("sigmoid_of_a_constant", [P, 1])
        flag = sb("not_solved", [1, 2], i32)
        zseq = sb("seq_pre_activation", [P, 2])
        diff = zsw.rearrange("p k c -> p (k c)")
        outt = xh3T

        banks = [ctx.enter_context(nc.psum_tensor(f"bank{i}", [P, CW], f32)) for i in range(8)]
        ST, MX, ZT, PJ = banks[0:3], banks[3:5], banks[5:7], banks[7]

        LN_BANKS = [banks[i] for i in (3, 4, 5, 6)]
        WX_BANKS = [banks[i] for i in (3, 4, 0, 1)]
        T2_BANKS = [banks[i] for i in (2, 7, 6, 5)]
        V_BANKS = T2_BANKS

        cs, as_ = Sems(sem, "conv"), Sems(sem, "attn")
        s_x = [sem(f"x_loaded_{b}") for b in range(B)]
        s_cw = sem("conv_weights_loaded")
        s_cproj = sem("conv_projection_loaded")
        s_cws = sem("conv_weights_split")
        s_xh = sem("x_high_parts_by_pool")
        s_x16 = sem("x_split_ready")
        s_tok = sem("tokens_loaded")
        s_w = sem("attn_weights_loaded")
        s_cst = sem("constants_loaded")
        s_ffn = sem("ffn_loaded")
        s_init = sem("dve_constants_ready")
        s_pinit = sem("pool_constants_ready")
        s_wt = sem("transposed_weights_in_psum")
        s_wtc = sem("transposed_weights_copied")
        s_am = sem("qk_and_projection_matrices_in_psum")
        s_ahi = sem("qk_matrix_high_ready")
        s_amd = sem("attn_matrices_ready")
        s_chain = sem("dve_chain")
        s_xt = sem("ln_values_ready")
        s_xtp = sem("ln_keys_in_psum")
        s_xs = sem("ln_keys_ready")
        s_ln3 = sem("ln3_statistics")
        s_l3 = sem("ln3_ready")
        s_tr = sem("ln3_transposes_in_psum")
        s_trc = sem("ln3_transposes_copied")
        s_t2 = sem("token_transposes_in_psum")
        s_t2c = sem("token_transposes_copied")
        s_wxp = sem("wx_in_psum")
        s_bn1 = sem("bn_means_local")
        s_bn2 = sem("bn_averages_in_psum")
        s_bn3 = sem("bn_averages_read")
        s_bn5 = sem("bn_affine_ready")
        s_wx = sem("wx_ready")
        s_wx16 = sem("wx16_ready")
        s_v = sem("sweep_products")
        s_z = sem("sweep_pre_activations")
        s_y = sem("sweep_chunks")
        s_df = sem("last_step_chunks")
        s_dm = sem("last_step_max_ready")
        s_dmt = sem("last_step_max_transposed")
        s_flag = sem("flag_ready")
        s_sv = sem("sequential_products")
        s_sz = sem("sequential_pre_activations")
        s_sy = sem("sequential_steps")
        s_out = sem("out_added")
        s_store = sem("out_stored")

        block = ctx.enter_context(nc.Block())
        CHAIN = [0]

        def chunk(y, k):
            return y[:, k // 2, 1 + (k % 2) * CW:1 + (k % 2 + 1) * CW]

        def by_head(t, r):
            return t[:].rearrange("p (g r c) -> p g r c", r=2, c=P)[:, :, r, :]

        def link(ins):
            CHAIN[0] += 1
            ins.then_inc(s_chain, 1)
            nc.vector.wait_ge(s_chain, CHAIN[0])


        def pe_prep_wait(ph, s, u, k):
            g = u * ph.nprep + k
            if not isinstance(g, int) or g >= MX_RING:
                nc.tensor.wait_ge(s.prep_used, g - MX_RING + 1)

        def pe_bank(ph, par, k):
            return MX[(par * ph.nprep + k) % MX_RING]

        def pe_queries(ph, s, u, par, b, h, k):
            pe_prep_wait(ph, s, u, k)
            o = pe_bank(ph, par, k)
            r = xs[:, ds(b * N + k * CW, CW)]
            nc.tensor.matmul(o[:], a_hi[:, ds(h * P, P)], r, start=True, stop=False)
            nc.tensor.matmul(o[:], a_lo[:, ds(h * P, P)], r, start=False, stop=True).then_inc(s.prep, 1)

        def pe_conv_prep(ph, s, u, par, k):
            pe_prep_wait(ph, s, u, k)
            if k == 0:
                nc.tensor.wait_ge(s_x16, u + 1)
            o = pe_bank(ph, par, k)

            def product(dst, stationary, moving):
                for part, (st, mo) in enumerate(zip(stationary, moving)):
                    ins = nc.tensor.matmul(dst, st, mo, start=part == 0, stop=part == 1)
                return ins

            if k < 4:
                cols = slice((k // 2) * P, (k // 2 + 1) * P)
                xk = x16[:, u * N + (k % 2) * CW:u * N + (k % 2 + 1) * CW]
                product(o[:], (cw_hi[:, cols], cw_lo[:, cols]), (xk, xk)).then_inc(s.prep, 1)
            else:
                for t in range(TPC):
                    g = u * N + ((k - 4) * TPC + t) * P
                    last = product(o[:, t * P:(t + 1) * P], (x16[:, g:g + P],) * 2,
                                   (cw_hi[:, 2 * P:3 * P], cw_lo[:, 2 * P:3 * P]))
                last.then_inc(s.prep, 1)

        def pe_rowmax(ph, s, u, par, keys, b, i):
            t, part, k0, w, diag = ph.maxes[i]
            pe_prep_wait(ph, s, u, ph.prep + i)
            o = pe_bank(ph, par, ph.prep + i)
            if ph.causal:
                nc.tensor.wait_ge(s.cast, u * NC + t // TPC + 1)
            else:
                nc.tensor.wait_ge(s.prep_used, u * ph.nprep + 4)
            ins = nc.tensor.matmul(o[:, 0:w], q_hi[par][:, t * P:(t + 1) * P], keys[:, ds(b * N + k0, w)],
                                   start=True, stop=not diag)
            if diag:
                ins = nc.tensor.matmul(o[:, w - P:w], identbf[:], masks[:, 1, :], start=False, stop=True)
            ins.then_inc(s.prep, 1)

        def pe_max_transpose(ph, s, u, par):
            k = ph.nprep - 1
            pe_prep_wait(ph, s, u, k)
            nc.tensor.wait_ge(s.rowmax, u + 1)
            nc.tensor.transpose(pe_bank(ph, par, k)[0:NT, 0:P], m8[par][:], cst[:, K_IDENT:K_IDENT + P]) \
                .then_inc(s.prep, 1)

        def pe_scores(ph, s, u, par, keys, b, n, first_unit):
            c, j, off, diag = ph.items[n]
            g = u * ph.n + n
            if first_unit and not ph.causal and n == 2:
                nc.tensor.wait_ge(s_ahi, 1)
            if not (first_unit and n < ST_RING):
                nc.tensor.wait_ge(s.probs, g - ST_RING + 1)
            if n == 0:
                nc.tensor.wait_ge(s.maxrow, 16 * (u + 1))
                nc.tensor.wait_ge(s.prep_used, (u + 1) * ph.nprep)
            o = ST[n % ST_RING] if ph.n % ST_RING == 0 else ST[(par_base(ph, u) + n) % ST_RING]
            lhs = keys[:, ds(b * N + j * P, P)]
            lo, hi = c * CW + off, (c + 1) * CW
            nc.tensor.matmul(o[:, off:CW], lhs, q_hi[par][:, lo:hi], start=True, stop=False)
            ins = nc.tensor.matmul(o[:, off:CW], lhs, q_lo[par][:, lo:hi], start=False, stop=not diag)
            if diag:
                ins = nc.tensor.matmul(o[:, off:off + P], identbf[:], masks[:, 0, :], start=False, stop=True)
            ins.then_inc(s.scores, 1)

        def par_base(ph, u):
            return u * ph.n if isinstance(u, int) else 0

        def slot(ph, u, n, ring):
            return n % ring if ph.n % ring == 0 else (par_base(ph, u) + n) % ring

        def pe_values(ph, s, u, values, b, n, first_unit):
            c, j, off, _ = ph.items[n]
            if first_unit and not ph.causal and n == 0:
                nc.tensor.wait_ge(s_amd, 1)
            if n == ph.first[c] and not first_unit:
                nc.tensor.wait_ge(s.zcopied, u * NC + c - 1)
            nc.tensor.wait_ge(s.probs, u * ph.n + n + 1)
            rs, rv = ph.rest_wait(s, u, n)
            nc.tensor.wait_ge(rs, rv)
            q = slot(ph, u, n, P_RING)
            lhs = values[:, ds((b * NT + j) * P, P)]
            nc.tensor.matmul(ZT[c][:, off:CW], lhs, p_hi[:, q, off:CW], start=(n == ph.first[c]), stop=False)
            nc.tensor.matmul(ZT[c][:, off:CW], lhs, p_lo[:, q, off:CW], start=False,
                             stop=(n == ph.last[c])).then_inc(s.values, 1)

        def pe_project(ph, s, u, pr, c, first_unit):
            nc.tensor.wait_ge(s.zcopied, u * NC + c + 1)
            if not (first_unit and c == 0):
                nc.tensor.wait_ge(s.scaled, u * NC + c)
            for t in range(TPC):
                last = nc.tensor.matmul(PJ[:, t * PO:(t + 1) * PO], zs[:, c, t * P:(t + 1) * P], pr,
                                        start=True, stop=True)
            last.then_inc(s.projected, 1)

        def value_slots(ph):
            return LAG

        def proj_slot(ph, c):
            return ph.last[c] + LAG + (3 if ph.causal else 1)

        def pe_unit(ph, s, u, par, keys, values, b, pr, prev, nxt, first, keys_slot=None, keys_batch=None,
                    tail=None):
            for n in range(ph.n):
                if tail is not None:
                    tail(n)
                if nxt is not None and n == 0:
                    nxt(n, 0)
                pe_scores(ph, s, u, par, keys, b, n, first)
                if nxt is not None and n > 0:
                    nxt(n, 0)
                if n >= LAG:
                    pe_values(ph, s, u, values, b, n - LAG, first)
                elif prev is not None:
                    pe_values(ph, s, u - 1, prev[0], prev[1], n - LAG + ph.n, prev[3])
                if nxt is not None:
                    nxt(n, 1)
                if n == keys_slot:
                    pe_xs_transposes(keys_batch)
                if keys_slot is not None and n == keys_slot + 2:
                    nc.tensor.wait_ge(s_xs, keys_batch + 1)
                for c in range(NC):
                    if n == proj_slot(ph, c):
                        pe_project(ph, s, u, pr, c, first)
                    if prev is not None and n == proj_slot(ph, c) - ph.n:
                        pe_project(ph, s, u - 1, prev[2], c, prev[3])

        def pe_drain(ph, s, u, values, b, pr):
            for n in range(ph.n, ph.n + LAG):
                pe_values(ph, s, u, values, b, n - LAG, False)
            pe_project(ph, s, u, pr, NC - 1, False)

        def a_slot_steps(ph, n):
            if ph.causal:
                table = {0: range(0, 2)}
                for i in range(6):
                    table[2 + i] = range(2 + 2 * i, 4 + 2 * i)
                table[9] = range(14, 15)
            else:
                table = {0: range(0, 2), 1: range(2, 4), 2: range(4, 6)}
                for i in range(8):
                    table[3 + i] = range(6 + 2 * i, 8 + 2 * i)
                table[12] = range(22, 23)
            return table.get(n, range(0))

        def half_of(steps, n, half):
            if n == 0:
                return [] if half else list(steps)
            return list(steps)[1:] if half else list(steps)[:1]

        def pe_a_step(ph, s, u, par, keys, b, h, k):
            if k < ph.prep:
                if ph.causal:
                    if h is not None:
                        pe_queries(ph, s, u, par, b, h, k)
                else:
                    pe_conv_prep(ph, s, u, par, k)
            elif k < ph.nprep - 1:
                pe_rowmax(ph, s, u, par, keys, b, k - ph.prep)
            else:
                pe_max_transpose(ph, s, u, par)

        def pr_of(h):
            return proj[:, ds(h * PO, PO)]

        def pe_attn_unit(u, par, last=False, first=False):
            b, h = u // H, u % H
            v = u + 1
            bn, hn = v // H, v % H
            nxt = None if last else (lambda n, half: [pe_a_step(ATTN, as_, v, 1 - par, xs, bn, hn, k)
                                                      for k in half_of(a_slot_steps(ATTN, n), n, half)])
            prev = None
            if not first:
                w = u - 1
                prev = (xt, w // H, pr_of(w % H), isinstance(w, int) and w == 0)
            pe_unit(ATTN, as_, u, par, xs, xt, b, pr_of(h), prev, nxt, first,
                    KEYS_SLOT3 if first else None, B - 1, pe_early_tail if last else None)

        def pe_transposes(dst, src, k):
            for t in range(TPC):
                g = ((k % 2) * TPC + t) * B * C + (k // 2) * P
                last = nc.tensor.transpose(dst[:, t * P:(t + 1) * P], src[:, g:g + P], cst[:, K_IDENT:K_IDENT + P])
            return last

        def pe_ln_transposes(k):
            nc.tensor.wait_ge(s_l3, k + 1)
            pe_transposes(LN_BANKS[k], xh3, k).then_inc(s_tr, 1)

        def pe_w(k):
            nc.tensor.wait_ge(s_trc, k + 1)
            nc.tensor.matmul(WX_BANKS[k][:], ffn_w[:, 0, :], xh3T[:, k * CW:(k + 1) * CW],
                             start=True, stop=True).then_inc(s_wxp, 1)

        def pe_early_tail(n):
            if n in (LAST_TR_SLOT, LAST_TR_SLOT + 1):
                pe_ln_transposes(n - LAST_TR_SLOT)
            if n == LAST_W_SLOT:
                nc.tensor.wait_ge(s_ffn, 32)
            if n in (LAST_W_SLOT, LAST_W_SLOT + 1):
                pe_w(n - LAST_W_SLOT)

        def pe_xs_transposes(b):
            pe = nc.tensor
            pe.wait_ge(s_xt, b + 1)
            pe.wait_ge(cs.scaled, (b + 2) * NC - 1 if b < B - 2 else B * NC)
            if b:
                pe.wait_ge(s_xs, b)
            for t in range(NT):
                last = nc.tensor.transpose(PT16[:, t * P:(t + 1) * P], xt[:, (b * NT + t) * P:(b * NT + t + 1) * P],
                                           ident16[:])
            last.then_inc(s_xtp, 1)

        PT16 = PJ[:].bitcast(f16)
        mv4 = mv[:].rearrange("p (t b) s -> p t b s", b=B)
        tok3 = tok[:].rearrange("p (t m) -> p t m", t=NT)

        @block.tensor
        def _(pe):
            pe.wait_ge(s_cws, 1)
            pe.wait_ge(s_x16, 1)
            for k in range(CONV.prep):
                pe_a_step(CONV, cs, 0, 0, cxs, 0, None, k)
            pe.wait_ge(s_cst, 16)
            pe.wait_ge(s_w, 64)
            for k in range(CONV.prep, CONV.nprep):
                pe_a_step(CONV, cs, 0, 0, cxs, 0, None, k)
                i, p = divmod(k - CONV.prep, H // 2)
                if i < 3:
                    ins = nc.tensor.matmul(banks[i][:, p * P:(p + 1) * P], (wq, wk, wv)[i][:, p * P:(p + 1) * P],
                                           cst[0:C, K_DIFF:K_DIFF + P], start=True, stop=True)
                    if p == H // 2 - 1:
                        ins.then_inc(s_wt, 1)
            pe.wait_ge(s_wtc, 3)
            for h in range(H):
                r = C * (h % 2)
                nc.tensor.matmul(banks[5 + h % 2][:, (h // 2) * P:(h // 2 + 1) * P], wqT[r:r + C, h // 2, :],
                                 wkT[r:r + C, h // 2, :], start=True, stop=True)
            for h in range(H):
                r = C * (h % 2)
                last = nc.tensor.matmul(banks[(7, 2)[h % 2]][:, (h // 2) * C:(h // 2 + 1) * C],
                                        wvT[r:r + C, h // 2, :], wo[r:r + C, h // 2, :],
                                        start=True, stop=True)
            last.then_inc(s_am, 1)
            pe.wait_ge(s_init, 1)
            pe.wait_ge(s_cproj, 16)
            for u in range(B):
                if u < B - 1:
                    def nxt(n, half, v=u + 1):
                        for k in half_of(a_slot_steps(CONV, n), n, half):
                            pe_a_step(CONV, cs, v, v % 2, cxs, v, None, k)
                else:
                    def nxt(n, half):
                        for k in half_of(a_slot_steps(ATTN, n), n, half):
                            pe_a_step(ATTN, as_, 0, 0, xs, 0, 0, k)
                prev = (cxt, u - 1, cproj[:], u - 1 == 0) if u else None
                pe_unit(CONV, cs, u, u % 2, cxs, cxt, u, cproj[:], prev, nxt, u == 0,
                        KEYS_SLOT if u >= 2 else None, u - 2)
            pe_drain(CONV, cs, B - 1, cxt, B - 1, cproj[:])
            pe_xs_transposes(2)

            pe_attn_unit(0, 0, first=True)
            with pe.Fori(0, (UNITS - 2) // 2) as i:
                pe_attn_unit(1 + 2 * i, 1)
                pe_attn_unit(2 + 2 * i, 0)
            pe_attn_unit(UNITS - 1, 1, last=True)
            pe_drain(ATTN, as_, UNITS - 1, xt, B - 1, pr_of(H - 1))

            pe.wait_ge(as_.added, UNITS * NC)
            pe_transposes(T2_BANKS[0], tok, 0).then_inc(s_t2, 1)
            pe_ln_transposes(2)
            pe_ln_transposes(3)
            pe_w(2)
            pe_w(3)
            pe.wait_ge(s_bn1, 1)
            nc.tensor.matmul(T2_BANKS[3][:, 0:2], cst[:, K_AVG:K_AVG + P], bmv[:], start=True, stop=True) \
                .then_inc(s_bn2, 1)
            for k in range(1, 4):
                if k == 3:
                    pe.wait_ge(s_bn3, 1)
                pe_transposes(T2_BANKS[k], tok, k).then_inc(s_t2, 1)

            for w in range(HALF_SWEEPS):
                for k in range(4):
                    if w == 0:
                        pe.wait_ge(s_wx16, k + 1)
                        pe.wait_ge(s_t2c, k + 1)
                    pe.wait_ge(s_y, 4 * w + k + 1)
                    yp = y16[w % 2][:, k // 2, (k % 2) * CW:(k % 2) * CW + CW]
                    nc.tensor.matmul(V_BANKS[k][:], ident16[:], wx16[:, k * CW:(k + 1) * CW], start=True, stop=False)
                    nc.tensor.matmul(V_BANKS[k][:], v16[:], yp, start=False, stop=True).then_inc(s_v, 1)
            for w in range(FULL_SWEEPS):
                for k in range(4):
                    pe.wait_ge(s_y, 4 * (HALF_SWEEPS + w) + k + 1)
                    yp = y32[w % 2][:, k // 2, (k % 2) * CW:(k % 2) * CW + CW]
                    nc.tensor.matmul(V_BANKS[k][:], ffn_w[:, 1, :], yp, start=True, stop=True).then_inc(s_v, 1)
            pe.wait_ge(s_dm, 1)
            nc.tensor.transpose(banks[4][0:1, 0:P], dmax[:, 4:5], cst[:, K_IDENT:K_IDENT + P]).then_inc(s_dmt, 1)
            pe.wait_ge(s_flag, 1)
            f = pe.value_load(flag[0:1, 0:1], min_val=0, max_val=1)
            yl = y32[FULL_SWEEPS % 2]
            with pe.If(f > 0):
                with pe.Fori(0, N) as t:
                    pe.wait_ge(s_sy, t + 1)
                    nc.tensor.matmul(banks[0][:, 0:2], ffn_w[:, 1, :], yl[:, :, ds(t, 1)].rearrange("p a b -> p (a b)"),
                                     start=True, stop=True).then_inc(s_sv, 1)

        def act_item(ph, s, u, n, first_unit, scale):
            c, j, off, _ = ph.items[n]
            g = u * ph.n + n
            nc.scalar.wait_ge(s.scores, g + 1)
            if not (first_unit and n < E_RING):
                rs, rv = ph.rest_wait(s, *ph.back(u, n, E_RING))
                nc.scalar.wait_ge(rs, rv)
            if not (first_unit and n < P_RING):
                nc.scalar.wait_ge(s.values, g - P_RING + 1)
            o = ST[slot(ph, u, n, ST_RING)]
            e, q = slot(ph, u, n, E_RING), slot(ph, u, n, P_RING)
            nc.scalar.activation(e32[:, e, off:CW], o[:, off:CW], ACT.Exp, scale=scale).then_inc(s.probs32, 1)
            nc.scalar.activation(p_hi[:, q, off:CW], o[:, off:CW], ACT.Exp, scale=scale).then_inc(s.probs, 1)

        def act_cast(ph, s, u, par, k):
            nc.scalar.wait_ge(s.prep, u * ph.nprep + k + 1)
            src = MX[(par * ph.nprep + k) % MX_RING]
            if ph.causal:
                dst = q_hi[par][:, k * CW:(k + 1) * CW]
            elif k < 2:
                dst = cxs[:, u * N + k * CW:u * N + (k + 1) * CW]
            elif k < 4:
                dst = q_hi[par][:, (k - 2) * CW:(k - 1) * CW]
            else:
                dst = cxt[:, (u * NT + (k - 4) * TPC) * P:(u * NT + (k - 3) * TPC) * P]
            nc.scalar.activation(dst, src[:], ACT.Copy).then_inc(s.cast, 1)

        def act_zcopy(ph, s, u, c, first_unit):
            nc.scalar.wait_ge(s.values, u * ph.n + ph.last[c] + 1)
            nc.scalar.activation(zs[:, c, :], ZT[c][:], ACT.Copy).then_inc(s.zcopied, 1)

        def zslot(ph, c):
            return ph.last[c] + LAG + 0

        def act_xs_copy(b):
            nc.scalar.wait_ge(s_xtp, b + 1)
            nc.scalar.activation(xs[:, b * N:(b + 1) * N], PT16, ACT.Copy).then_inc(s_xs, 1)

        def act_unit(ph, s, u, par, first, prev_first, has_prev, nxt, scale, keys_slot=None, keys_batch=None,
                     first_attn=False, last=False):
            for n in range(ph.n):
                if last and n in (LAST_TR_SLOT + 1, LAST_TR_SLOT + 2):
                    act_ln_copy(n - LAST_TR_SLOT - 1)
                if nxt:
                    for k in a_slot_steps(ph, n):
                        if k < ph.prep:
                            act_cast(ph, s, u + 1, 1 - par, k)
                if first_attn:
                    for k in a_slot_steps(ATTN, n):
                        if k < ATTN.prep:
                            act_cast(ATTN, as_, 0, 0, k)
                act_item(ph, s, u, n, first, scale)
                if n == keys_slot:
                    act_xs_copy(keys_batch)
                for c in range(NC):
                    if n == zslot(ph, c):
                        act_zcopy(ph, s, u, c, first)
                    if has_prev and n == zslot(ph, c) - ph.n:
                        act_zcopy(ph, s, u - 1, c, prev_first)

        def act_ln_copy(k):
            nc.scalar.wait_ge(s_tr, k + 1)
            nc.scalar.activation(xh3T[:, k * CW:(k + 1) * CW], LN_BANKS[k][:], ACT.Copy).then_inc(s_trc, 1)

        @block.scalar
        def _(act):
            act.dma_start(cst[:], const).then_inc(s_cst, 16)
            act.dma_start(tok[:], x_tm).then_inc(s_tok, 16)
            for i, (t, src) in enumerate(((wq, w_q), (wk, w_k), (wv, w_v))):
                act.dma_start(t[:], src).then_inc(s_w, 16)
            act.dma_start(wo[:], w_o.rearrange("(g p) c -> p g c", p=P)).then_inc(s_w, 16)
            for k in range(CONV.prep):
                act_cast(CONV, cs, 0, 0, k)
            for t, bk in ((wqT, 0), (wkT, 1), (wvT, 2)):
                act.wait_ge(s_wt, bk + 1)
                nc.scalar.activation(t[:].rearrange("p g c -> p (g c)"), banks[bk][:], ACT.Copy).then_inc(s_wtc, 1)
            act.wait_ge(s_am, 1)
            for r in range(2):
                nc.scalar.activation(by_head(a_hi, r), banks[5 + r][:].rearrange("p (g c) -> p g c", c=P), ACT.Copy)
                ins = nc.scalar.activation(proj[:].rearrange("p (g r c) -> p g r c", r=2, c=PO)[:, :, r, 0:C],
                                           banks[(7, 2)[r]][:, 0:H // 2 * C].rearrange("p (g c) -> p g c", c=C), ACT.Copy)
            ins.then_inc(s_ahi, 1)
            for u in range(B):
                act_unit(CONV, cs, u, u % 2, u == 0, u == 1, u > 0, u < B - 1, 1.0,
                         KEYS_SLOT if u >= 2 else None, u - 2, first_attn=u == B - 1)
            act_zcopy(CONV, cs, B - 1, NC - 1, False)
            act_xs_copy(2)
            act.wait_ge(cs.values, B * CONV.n)
            act_unit(ATTN, as_, 0, 0, True, False, False, True, SCALE, KEYS_SLOT3, B - 1)
            with act.Fori(0, (UNITS - 2) // 2) as i:
                act_unit(ATTN, as_, 1 + 2 * i, 1, False, True, True, True, SCALE)
                act_unit(ATTN, as_, 2 + 2 * i, 0, False, False, True, True, SCALE)
            act_unit(ATTN, as_, UNITS - 1, 1, False, False, True, False, SCALE, last=True)
            act_zcopy(ATTN, as_, UNITS - 1, NC - 1, False)
            nc.scalar.activation(sig_table[:], cst[:, 0:1], ACT.Sigmoid)
            for k in range(2, 4):
                act_ln_copy(k)
            for k in range(4):
                act.wait_ge(s_t2, k + 1)
                nc.scalar.activation(t2T[:, k * CW:(k + 1) * CW], T2_BANKS[k][:], ACT.Copy).then_inc(s_t2c, 1)
            act.wait_ge(s_bn5, 1)
            for k in range(4):
                nc.scalar.activation(y16[0][:, k // 2, 1 + (k % 2) * CW:1 + (k % 2) * CW + CW],
                                     WX_BANKS[k][:], ACT.Sigmoid, scale=bwk[:, 5:6], bias=bwk[:, 6:7]).then_inc(s_y, 1)
            for w in range(HALF_SWEEPS):
                dst = y16[(w + 1) % 2] if w < HALF_SWEEPS - 1 else y32[0]
                for k in range(4):
                    act.wait_ge(s_v, 4 * w + k + 1)
                    if w >= 1:
                        act.wait_ge(s_v, min(4 * w + k + 1, 4 * (w - 1) + k + 2))
                    nc.scalar.activation(dst[:, k // 2, 1 + (k % 2) * CW:1 + (k % 2) * CW + CW],
                                         V_BANKS[k][:], ACT.Sigmoid).then_inc(s_y, 1)
            for w in range(FULL_SWEEPS):
                dst = y32[(w + 1) % 2]
                for k in range(4):
                    act.wait_ge(s_z, 4 * w + k + 1)
                    nc.scalar.activation(dst[:, k // 2, 1 + (k % 2) * CW:1 + (k % 2) * CW + CW],
                                         zsw[:, k, :], ACT.Sigmoid).then_inc(s_y, 1)
            act.wait_ge(s_flag, 1)
            f = act.value_load(flag[0:1, 0:1], min_val=0, max_val=1)
            yl = y32[FULL_SWEEPS % 2]
            with act.If(f > 0):
                with act.Fori(0, N) as t:
                    act.wait_ge(s_sz, t + 1)
                    nc.scalar.activation(yl[:, :, ds(t + 1, 1)].rearrange("p a b -> p (a b)"), zseq[:],
                                         ACT.Sigmoid).then_inc(s_sy, 1)

        def rest_item(eng, ph, s, u, n, first_unit):
            off = ph.items[n][2]
            g = u * ph.n + n
            eng.wait_ge(s.probs, g + 1)
            if not (first_unit and n < P_RING):
                eng.wait_ge(s.values, g - P_RING + 1)
            e, q = slot(ph, u, n, E_RING), slot(ph, u, n, P_RING)
            rs, _ = ph.rest_wait(s, u, n)
            eng.tensor_tensor(out=p_lo[:, q, off:CW], in0=e32[:, e, off:CW], in1=p_hi[:, q, off:CW],
                              op=ALU.subtract).then_inc(rs, 1)

        def dve_a_step(ph, s, u, par, k):
            dve = nc.vector
            src = MX[(par * ph.nprep + k) % MX_RING]
            dve.wait_ge(s.prep, u * ph.nprep + k + 1)
            mxs = (amx if ph.causal else cmx)[par]
            if k < ph.prep:
                dve.wait_ge(s.cast, u * ph.prep + k + 1)
                if ph.causal:
                    a = q_hi[par][:, k * CW:(k + 1) * CW]
                    nc.vector.tensor_tensor(out=q_lo[par][:, k * CW:(k + 1) * CW], in0=src[:], in1=a,
                                            op=ALU.subtract).then_inc(s.prep_used, 1)
                elif k < 2:
                    a = cxs[64:96, u * N + k * CW:u * N + (k + 1) * CW]
                    nc.vector.memset(cxs[0:1, u * N + k * CW:u * N + (k + 1) * CW], 1.0)
                    nc.vector.tensor_tensor(out=a, in0=src[64:96, :], in1=a, op=ALU.subtract).then_inc(s.prep_used, 1)
                elif k < 4:
                    a = q_hi[par][:, (k - 2) * CW:(k - 1) * CW]
                    nc.vector.tensor_tensor(out=q_lo[par][:, (k - 2) * CW:(k - 1) * CW], in0=src[:], in1=a,
                                            op=ALU.subtract).then_inc(s.prep_used, 1)
                else:
                    g = (u * NT + (k - 4) * TPC) * P
                    a = cxt[:, g:g + CW].rearrange("p (t c) -> p t c", t=TPC)
                    nc.vector.memset(a[:, :, 0:1], 1.0)
                    nc.vector.tensor_tensor(out=a[:, :, 64:96], in0=src[:].rearrange("p (t c) -> p t c", t=TPC)[:, :, 64:96],
                                            in1=a[:, :, 64:96], op=ALU.subtract).then_inc(s.prep_used, 1)
            elif k < ph.nprep - 1:
                t, part, k0, w, diag = ph.maxes[k - ph.prep]
                nc.vector.reduce_max(mxs[:, t, part:part + 1], src[:, 0:w], AX).then_inc(s.prep_used, 1)
            else:
                nc.vector.tensor_scalar(mrow[par][:], src[0:NT, 0:P], -1.0, None, ALU.mult).then_inc(s.prep_used, 1)

        def dve_rowmax(ph, s, u, par):
            mxs = (amx if ph.causal else cmx)[par]
            nc.vector.wait_ge(s.prep_used, (u + 1) * ph.nprep - 1)
            nc.vector.reduce_max(m8[par][:], mxs[:], AX).then_inc(s.rowmax, 1)

        def dve_scale(ph, s, u, c, first_unit):
            dve = nc.vector
            dve.wait_ge(s.projected, u * NC + c + 1)
            pj = PJ[:, 0:TPC * PO].rearrange("p (t c) -> p t c", c=PO)
            nc.vector.reciprocal(rden[:, c, :], pj[:, :, C:PO].rearrange("p t c -> p (t c)")).then_inc(s.recip, 1)
            if not first_unit:
                dve.wait_ge(s.added, u * NC + c - 1)
            dve.wait_ge(s.recip, u * NC + c + 1)
            nc.vector.tensor_tensor(out=scaled[:, c, :, :], in0=pj[:, :, 0:C],
                                    in1=rden[:, c, :].unsqueeze(2).to_broadcast([P, TPC, C]),
                                    op=ALU.mult).then_inc(s.scaled, 1)

        def pool_add(ph, s, u, b, c, first_unit):
            nc.gpsimd.wait_ge(s.scaled, u * NC + c + 1)
            if not (first_unit and c == 0):
                nc.gpsimd.wait_ge(s.added, u * NC + c)
            dst = tok3[:, c * TPC:(c + 1) * TPC, ds(b * C, C)]
            nc.gpsimd.tensor_tensor(out=dst, in0=scaled[:, c, :, :], in1=dst, op=ALU.add).then_inc(s.added, 1)

        def dve_drain(ph, s, u, b):
            for n in range(ph.n - REST_LAG, ph.n):
                if n in ph.dve_items:
                    rest_item(nc.vector, ph, s, u, n, False)
            dve_scale(ph, s, u, NC - 1, False)

        def rowmax_slot(ph):
            return 7 if ph.causal else 11

        def add_slot(ph, c):
            return ph.last[c] + LAG + (3 if ph.causal else 1)

        def dve_unit(ph, s, u, par, b, bprev, first, prev_first, has_prev, nxt, ln1=None, first_attn=False,
                     last=False):
            for n in range(ph.n):
                if last:
                    dve_early_tail(n)
                if first_attn:
                    for k in a_slot_steps(ATTN, n):
                        dve_a_step(ATTN, as_, 0, 0, k)
                    if n == rowmax_slot(ATTN):
                        dve_rowmax(ATTN, as_, 0, 0)
                ln3_slots = (0, 1, 2) if last else LN3_SLOTS
                if ph.causal and n == ln3_slots[1]:
                    nc.vector.wait_ge(s_ln3, 3 * u + 1)
                    nc.vector.memset(wait_carrier[:], 0.0)
                if nxt:
                    for k in a_slot_steps(ph, n):
                        dve_a_step(ph, s, u + 1, 1 - par, k)
                    if n == rowmax_slot(ph):
                        dve_rowmax(ph, s, u + 1, 1 - par)
                if n - REST_LAG in ph.dve_items:
                    rest_item(nc.vector, ph, s, u, n - REST_LAG, first)
                if has_prev and n - REST_LAG + ph.n in ph.dve_items:
                    rest_item(nc.vector, ph, s, u - 1, n - REST_LAG + ph.n, prev_first)
                for c in range(NC):
                    if n == add_slot(ph, c):
                        dve_scale(ph, s, u, c, first)
                    if has_prev and n == add_slot(ph, c) - ph.n:
                        dve_scale(ph, s, u - 1, c, prev_first)
                if ln1 is not None and ln1[1] <= n < ln1[1] + LN_STEPS:
                    dve_ln1(ln1[0], n - ln1[1])
                if ph.causal and n in ln3_slots:
                    dve_ln3_stats(u, ln3_slots.index(n), last)

        def dve_rsqrt(r, v, w):
            link(nc.vector.tensor_scalar(r.bitcast(i32), v.bitcast(i32), -0.5, 1597463007.0, ALU.mult, ALU.add))
            for _ in range(3):
                link(nc.vector.tensor_tensor(out=w, in0=r, in1=v, op=ALU.mult))
                link(nc.vector.scalar_tensor_tensor(out=w, in0=w, scalar=-0.5, in1=r, op0=ALU.mult, op1=ALU.mult))
                link(nc.vector.scalar_tensor_tensor(out=r, in0=w, scalar=1.5, in1=r, op0=ALU.add, op1=ALU.mult))

        LN_STEPS = 6

        def dve_ln1(b, step):
            x3 = xh[:].rearrange("p (t c) -> p t c", c=C)
            v3 = xt[:, b * NT * P:(b + 1) * NT * P].rearrange("p (t c) -> p t c", c=P)
            if step == 0:
                nc.vector.wait_ge(cs.added, (b + 1) * NC)
                for t in range(NT):
                    ins = nc.vector.bn_stats(stats[:, t, :], tok[:, (t * B + b) * C:(t * B + b + 1) * C])
                link(ins)
            elif step == 1:
                for t in range(NT):
                    ins = nc.vector.bn_aggr(mv[:, t, :], stats[:, t, :])
                link(ins)
                link(nc.vector.tensor_scalar_add(var_eps[:, 0:NT], mv[:, 0:NT, 1:2].rearrange("p t c -> p (t c)"), LN_EPS))
            elif step == 2:
                dve_rsqrt(rstd[:, 0:NT], var_eps[:, 0:NT], nwt[:, 0:NT])
            elif step == 3:
                for t in range(NT):
                    ins = nc.vector.tensor_scalar(xh[:, t * C:(t + 1) * C], tok[:, (t * B + b) * C:(t * B + b + 1) * C],
                                                  mv[:, t, 0:1], rstd[:, t:t + 1], ALU.subtract, ALU.mult)
                link(ins)
            elif step == 4:
                link(nc.vector.tensor_copy(v3[:, :, 0:C], x3))
            else:
                link(nc.vector.tensor_tensor(out=v3[:, :, C:P], in0=x3, in1=v3[:, :, 0:C], op=ALU.subtract))
                nc.vector.memset(v3[:, :, 0:1], 1.0)
                nc.vector.memset(v3[:, :, C:C + 1], 0.0).then_inc(s_xt, 1)

        def dve_ln3_stats(u, part, last):
            b, t = (u // H + B - 1) % B, u % NT
            if part == 0:
                if last:
                    nc.vector.wait_ge(as_.added, (B - 1) * H * NC)
                elif not (isinstance(u, int) and u == 0):
                    nc.vector.wait_ge(as_.added, u * NC)
                nc.vector.bn_stats(stats[:, 0, :], tok[:, ds(t * (B * C) + b * C, C)]).then_inc(s_ln3, 1)
            elif part == 1:
                nc.vector.bn_aggr(mv_one[:], stats[:, 0, :]).then_inc(s_ln3, 1)
            else:
                nc.vector.wait_ge(s_ln3, 3 * u + 2)
                nc.vector.tensor_copy(mv[:, ds(t * B + b, 1), :].rearrange("p a c -> p (a c)"),
                                      mv_one[:]).then_inc(s_ln3, 1)

        def last_stats(c):
            nc.vector.wait_ge(as_.added, (UNITS - 1) * NC + c + 1)
            for t in range(c * TPC, (c + 1) * TPC):
                ins = nc.vector.bn_stats(stats[:, t, :], tok[:, (t * B + B - 1) * C:(t + 1) * B * C])
            link(ins)
            for t in range(c * TPC, (c + 1) * TPC):
                ins = nc.vector.bn_aggr(mv[:, t * B + B - 1, :], stats[:, t, :])
            return ins

        def ln3_rstd(b0, b1):
            v, r, w = (x[:].rearrange("p (t b) -> p t b", b=B)[:, :, b0:b1] for x in (var_eps, rstd, nwt))
            link(nc.vector.tensor_scalar_add(v, mv4[:, :, b0:b1, 1], LN_EPS))
            dve_rsqrt(r, v, w)

        def ln3_apply(k, b0, b1):
            tiles = slice(k * TPC, (k + 1) * TPC)
            shape = [P, TPC, b1 - b0, C]
            x, y = (a[:].rearrange("p (t b c) -> p t b c", b=B, c=C)[:, tiles, b0:b1, :] for a in (tok, xh3))
            mean = mv4[:, tiles, b0:b1, 0:1].to_broadcast(shape)
            scale = rstd[:].rearrange("p (t b) -> p t b", b=B)[:, tiles, b0:b1].unsqueeze(3).to_broadcast(shape)
            link(nc.vector.tensor_tensor(out=y, in0=x, in1=mean, op=ALU.subtract))
            return nc.vector.tensor_tensor(out=y, in0=y, in1=scale, op=ALU.mult)

        def dve_early_tail(n):
            if n == 3:
                nc.vector.wait_ge(s_ln3, 3 * UNITS)
                ln3_rstd(0, B - 1)
            elif n in (4, 5):
                ln3_apply(n - 4, 0, 2).then_inc(s_l3, 1)
            elif n == 6:
                ln3_apply(0, 2, 3)
            elif n == 7:
                ln3_apply(1, 2, 3)
            elif n == ATTN.n - 1:
                for k in range(2):
                    bn_partial(k)

        def bn_partial(k):
            nc.vector.wait_ge(s_wxp, k + 1)
            return nc.vector.bn_stats(bst[:, k, :], WX_BANKS[k][:])

        @block.vector
        def _(dve):
            dve.wait_ge(s_cw, 16)
            link(nc.vector.tensor_copy(cw_hi[:], cw[:]))
            nc.vector.tensor_tensor(out=cw_lo[:], in0=cw[:], in1=cw_hi[:], op=ALU.subtract).then_inc(s_cws, 1)
            dve.wait_ge(s_x[0], 32)
            link(nc.vector.tensor_copy(x16[:, 0:N], xc[:, 0:N]))
            nc.vector.tensor_tensor(out=x16[C:P, 0:N], in0=xc[C:P, 0:N], in1=x16[C:P, 0:N],
                                    op=ALU.subtract).then_inc(s_x16, 1)
            dve.wait_ge(s_cst, 16)
            nc.vector.tensor_copy(ident16[:], cst[:, K_IDENT:K_IDENT + P])
            nc.vector.tensor_copy(identbf[:], cst[:, K_IDENT:K_IDENT + P])
            nc.vector.tensor_copy(masks[:].rearrange("p a c -> p (a c)"), cst[:, K_MASK_T:K_MASK_T + 2 * P]) \
                .then_inc(s_init, 1)
            for i in range(2):
                nc.vector.memset(amx[i][:], -3e38)
                nc.vector.memset(y16[i][:, :, 0:1], 0.0)
                nc.vector.memset(y32[i][:, :, 0:1], 0.0)
            pj3 = proj[:].rearrange("p (h c) -> p h c", c=PO)
            link(nc.vector.memset(pj3[:, :, C:PO], 0.0))
            link(nc.vector.memset(pj3[0:1, :, C:PO], 1.0))
            dve.wait_ge(s_tok, 16)
            for k in range(CONV.nprep):
                if k == CONV.nprep - 1:
                    dve_rowmax(CONV, cs, 0, 0)
                dve_a_step(CONV, cs, 0, 0, k)
            dve.wait_ge(s_ahi, 1)
            for r in range(2):
                ins = nc.vector.tensor_tensor(out=by_head(a_lo, r), in0=banks[5 + r][:].rearrange("p (g c) -> p g c", c=P),
                                              in1=by_head(a_hi, r), op=ALU.subtract)
            ins.then_inc(s_amd, 1)
            for u in range(B):
                dve_unit(CONV, cs, u, u % 2, u, u - 1, u == 0, u == 1, u > 0, u < B - 1,
                         ln1=(u - 1, LN1_SLOT) if u else None, first_attn=u == B - 1)
            dve_drain(CONV, cs, B - 1, B - 1)
            dve_unit(ATTN, as_, 0, 0, 0, 0, True, False, False, True, ln1=(B - 1, 1))
            with dve.Fori(0, (UNITS - 2) // 2) as i:
                dve_unit(ATTN, as_, 1 + 2 * i, 1, (1 + 2 * i) // H, (2 * i) // H, False, True, True, True)
                dve_unit(ATTN, as_, 2 + 2 * i, 0, (2 + 2 * i) // H, (1 + 2 * i) // H, False, False, True, True)
            dve_unit(ATTN, as_, UNITS - 1, 1, B - 1, B - 1, False, False, True, False, last=True)
            link(last_stats(0))
            dve_drain(ATTN, as_, UNITS - 1, B - 1)
            link(last_stats(1))
            ln3_rstd(B - 1, B)
            for k in range(2):
                ln3_apply(k, B - 1, B).then_inc(s_l3, 1)
            nc.vector.tensor_copy(v16[:], ffn_w[:, 1, :])
            bn_partial(2)
            link(bn_partial(3))
            nc.vector.bn_aggr(bmv[:], bst[:].rearrange("p k c -> p (k c)")).then_inc(s_bn1, 1)
            dve.wait_ge(s_bn1, 1)
            dve.wait_ge(s_bn2, 1)
            avg = T2_BANKS[3]
            nc.vector.tensor_copy(bwk[:, 0:1], avg[:, 0:1])
            nc.vector.tensor_tensor(out=bwk[:, 1:2], in0=bmv[:, 0:1], in1=avg[:, 0:1], op=ALU.subtract)
            nc.vector.tensor_scalar_add(bwk[:, 2:3], avg[:, 1:2], 1e-5).then_inc(s_bn3, 1)
            dve.wait_ge(s_bn3, 1)
            link(nc.vector.scalar_tensor_tensor(out=bwk[:, 3:4], in0=bwk[:, 1:2], scalar=bwk[:, 1:2], in1=bwk[:, 2:3],
                                                op0=ALU.mult, op1=ALU.add))
            dve_rsqrt(bwk[:, 4:5], bwk[:, 3:4], bwk[:, 7:8])
            link(nc.vector.tensor_tensor(out=bwk[:, 5:6], in0=bwk[:, 4:5], in1=gbt[:, 0:1], op=ALU.mult))
            link(nc.vector.tensor_tensor(out=bwk[:, 7:8], in0=bwk[:, 5:6], in1=bwk[:, 0:1], op=ALU.mult))
            nc.vector.tensor_tensor(out=bwk[:, 6:7], in0=gbt[:, 1:2], in1=bwk[:, 7:8],
                                    op=ALU.subtract).then_inc(s_bn5, 1)
            dve.wait_ge(s_bn5, 1)
            for dst, done in ((wx16, s_wx16), (wx, s_wx)):
                for k in range(4):
                    dve.wait_ge(s_y, k + 1)
                    nc.vector.tensor_scalar(dst[:, k * CW:(k + 1) * CW], WX_BANKS[k][:], bwk[:, 5:6], bwk[:, 6:7],
                                            ALU.mult, ALU.add).then_inc(done, 1)
            ya, yb = y32[(FULL_SWEEPS - 1) % 2], y32[FULL_SWEEPS % 2]
            ALL = 4 * (HALF_SWEEPS + FULL_SWEEPS)

            def out_add(k):
                dve.wait_ge(s_y, ALL + k + 1)
                nc.vector.tensor_tensor(out=outt[:, k * CW:(k + 1) * CW], in0=t2T[:, k * CW:(k + 1) * CW],
                                        in1=chunk(yb, k), op=ALU.add).then_inc(s_out, 1)

            def step_max(k):
                dve.wait_ge(s_df, k + 1)
                return nc.vector.tensor_reduce(out=dmax[:, k:k + 1], in_=diff[:, k * CW:(k + 1) * CW], axis=AX,
                                               op=ALU.max, apply_absolute_value=True)

            dve.wait_ge(s_wx, 4)
            for w in range(FULL_SWEEPS):
                for k in range(4):
                    dve.wait_ge(s_v, 4 * (HALF_SWEEPS + w) + k + 1)
                    if w:
                        dve.wait_ge(s_y, 4 * (HALF_SWEEPS + w) + k + 1)
                    nc.vector.tensor_tensor(out=zsw[:, k, :], in0=V_BANKS[k][:], in1=wx[:, k * CW:(k + 1) * CW],
                                            op=ALU.add).then_inc(s_z, 1)
                    if w == FULL_SWEEPS - 1 and k == 2:
                        out_add(0)
            step_max(0)
            for k in range(1, 4):
                out_add(k)
                ins = step_max(k)
            link(ins)
            nc.vector.reduce_max(dmax[:, 4:5], dmax[:, 0:4], AX).then_inc(s_dm, 1)
            dve.wait_ge(s_dmt, 1)
            link(nc.vector.reduce_max(dmax[0:1, 5:6], banks[4][0:1, 0:P], AX))
            nc.vector.tensor_scalar(flag[0:1, 0:1], dmax[0:1, 5:6], RESIDUAL_LIMIT, None, ALU.is_gt).then_inc(s_flag, 1)
            dve.wait_ge(s_flag, 1)
            f = dve.value_load(flag[0:1, 0:1], min_val=0, max_val=1)
            with dve.If(f > 0):
                nc.vector.memset(diff[:, 0:1], 0.0).then_inc(s_sy, 1)
                wx2 = wx[:].rearrange("p (a n) -> p a n", a=2)
                with dve.Fori(0, N) as t:
                    dve.wait_ge(s_sv, t + 1)
                    nc.vector.tensor_tensor(out=zseq[:], in0=banks[0][:, 0:2],
                                            in1=wx2[:, :, ds(t, 1)].rearrange("p a b -> p (a b)"),
                                            op=ALU.add).then_inc(s_sz, 1)
                dve.wait_ge(s_sy, N + 1)
                dve.wait_ge(s_store, 4 * 16)
                for k in range(4):
                    nc.vector.tensor_tensor(out=outt[:, k * CW:(k + 1) * CW], in0=t2T[:, k * CW:(k + 1) * CW],
                                            in1=chunk(yb, k), op=ALU.add).then_inc(s_out, 1)

        def pool_unit(ph, s, u, b, bprev, first, prev_first, has_prev):
            for n in range(ph.n):
                if n in ph.pool_items:
                    rest_item(nc.gpsimd, ph, s, u, n, first)
                for c in range(NC):
                    if n == add_slot(ph, c):
                        pool_add(ph, s, u, b, c, first)
                    if has_prev and n == add_slot(ph, c) - ph.n:
                        pool_add(ph, s, u - 1, bprev, c, prev_first)

        @block.gpsimd
        def _(pool):
            for b in range(1, B):
                pool.wait_ge(s_x[b], 32)
                pool.wait_ge(s_x16, b)
                nc.gpsimd.tensor_copy(x16[:, b * N:(b + 1) * N], xc[:, b * N:(b + 1) * N]).then_inc(s_xh, 1)
                pool.wait_ge(s_xh, b)
                nc.gpsimd.tensor_tensor(out=x16[C:P, b * N:(b + 1) * N], in0=xc[C:P, b * N:(b + 1) * N],
                                        in1=x16[C:P, b * N:(b + 1) * N], op=ALU.subtract).then_inc(s_x16, 1)
            pool.wait_ge(s_x16, B)
            pool.wait_ge(s_tok, 16)
            for u in range(B):
                pool_unit(CONV, cs, u, u, u - 1, u == 0, u == 1, u > 0)
            pool_add(CONV, cs, B - 1, B - 1, NC - 1, False)
            pool.wait_ge(cs.added, B * NC)
            pool_unit(ATTN, as_, 0, 0, 0, True, False, False)
            with pool.Fori(0, (UNITS - 2) // 2) as i:
                pool_unit(ATTN, as_, 1 + 2 * i, (1 + 2 * i) // H, (2 * i) // H, False, True, True)
                pool_unit(ATTN, as_, 2 + 2 * i, (2 + 2 * i) // H, (1 + 2 * i) // H, False, False, True)
            pool_unit(ATTN, as_, UNITS - 1, B - 1, B - 1, False, False, True)
            pool_add(ATTN, as_, UNITS - 1, B - 1, NC - 1, False)
            ya, yb = y32[(FULL_SWEEPS - 1) % 2], y32[FULL_SWEEPS % 2]
            for k in range(4):
                pool.wait_ge(s_y, 4 * (HALF_SWEEPS + FULL_SWEEPS) + k + 1)
                nc.gpsimd.tensor_tensor(out=diff[:, k * CW:(k + 1) * CW], in0=chunk(ya, k), in1=chunk(yb, k),
                                        op=ALU.subtract).then_inc(s_df, 1)

        def sp_maxrow(ph, s, u, par):
            nc.sync.wait_ge(s.prep_used, (u + 1) * ph.nprep)
            nc.sync.dma_start(q_hi[par][0:1, :], mrow[par][:]).then_inc(s.maxrow, 16)

        @block.sync
        def _(sp):
            sp.dma_start(cw[:], conv_w).then_inc(s_cw, 16)
            for b in range(B):
                for r in range(2):
                    sp.dma_start(xc[r * C:(r + 1) * C, b * N:(b + 1) * N], x_cm[b]).then_inc(s_x[b], 16)
            sp.dma_start(cproj[:], conv_proj).then_inc(s_cproj, 16)
            sp.dma_start(ffn_w[:], ffn).then_inc(s_ffn, 16)
            sp.dma_start(gbt[:], gb).then_inc(s_ffn, 16)
            for u in range(B):
                sp_maxrow(CONV, cs, u, u % 2)
            sp_maxrow(ATTN, as_, 0, 0)
            with sp.Fori(0, (UNITS - 2) // 2) as i:
                sp_maxrow(ATTN, as_, 1 + 2 * i, 1)
                sp_maxrow(ATTN, as_, 2 + 2 * i, 0)
            sp_maxrow(ATTN, as_, UNITS - 1, 1)

            def store(k):
                sp.dma_start(out[(k // 2) * P:(k // 2 + 1) * P, (k % 2) * CW:(k % 2 + 1) * CW],
                             outt[:, k * CW:(k + 1) * CW]).then_inc(s_store, 16)

            for k in range(4):
                sp.wait_ge(s_out, k + 1)
                store(k)
            sp.wait_ge(s_store, 4 * 16)
            sp.wait_ge(s_flag, 1)
            f = sp.value_load(flag[0:1, 0:1], min_val=0, max_val=1)
            with sp.If(f > 0):
                for k in range(4):
                    sp.wait_ge(s_out, 4 + k + 1)
                    store(k)
                sp.wait_ge(s_store, 8 * 16)


def kernel(x, L0_conv_wq, L0_conv_wk, L0_conv_wv, L0_conv_wo, L1_attn_Wq, L1_attn_Wk, L1_attn_Wv, L1_attn_Wo,
           L1_ffn_W, L1_ffn_V, L1_ffn_gamma, L1_ffn_beta):
    import numpy as np
    import concourse.bacc as bacc
    from concourse.bass_utils import run_bass_kernel_spmd as run

    x = np.asarray(x)
    f = x.dtype
    x_cm = np.ascontiguousarray(x.reshape(B, C, N))
    x_tm = np.ascontiguousarray(x_cm.reshape(B, C, NT, P).transpose(3, 2, 0, 1).reshape(P, NT * B * C))
    conv_w = np.zeros((P, 3, P), f)
    for i, w in enumerate((L0_conv_wq, L0_conv_wk, L0_conv_wv)):
        conv_w[:, i, MC:2 * MC] = conv_w[:, i, 2 * MC:3 * MC] = np.tile(np.asarray(w).T, (2, 1))
    conv_proj = np.zeros((P, PO), f)
    conv_proj[MC:2 * MC, 0:C] = conv_proj[2 * MC:3 * MC, 0:C] = np.asarray(L0_conv_wo).T
    conv_proj[0, C] = 1.0
    ffn = np.zeros((P, 2, P), f)
    for i, w in enumerate((L1_ffn_W, L1_ffn_V)):
        ffn[0:C, i, 0:C] = ffn[C:P, i, C:P] = np.asarray(w).T
    gb = np.stack([np.tile(np.asarray(L1_ffn_gamma), 2), np.tile(np.asarray(L1_ffn_beta), 2)], axis=1)
    const = np.zeros((P, CONST_COLS), f)
    r, c = np.arange(P)[:, None], np.arange(P)[None, :]
    const[:, K_IDENT:K_IDENT + P] = r == c
    const[:, K_AVG:K_AVG + P] = np.where(r % C == c % C, 0.5, 0.0)
    const[:, K_MASK_T:K_MASK_T + P] = np.where(c < r, NEG, 0.0)
    const[:, K_MASK_R:K_MASK_R + P] = np.where(c > r, NEG, 0.0)
    const[:, K_DIFF:K_DIFF + P] = np.where(c % C == 0, 0.0, np.where(r == c % C, 1.0, np.where(r == 0, -1.0, 0.0)))

    arrays = dict(x_cm=x_cm, x_tm=x_tm, conv_w=conv_w.reshape(P, 3 * P), conv_proj=conv_proj,
                  w_q=np.asarray(L1_attn_Wq), w_k=np.asarray(L1_attn_Wk), w_v=np.asarray(L1_attn_Wv),
                  w_o=np.asarray(L1_attn_Wo), ffn=ffn, gb=gb, const=const)
    arrays = {k: np.ascontiguousarray(v) for k, v in arrays.items()}
    nc = bacc.Bacc("TRN2", target_bir_lowering=False, num_devices=1)
    aps = {k: nc.dram_tensor(f"in_{k}", v.shape, mybir.dt.from_np(v.dtype), kind="ExternalInput").ap()
           for k, v in arrays.items()}
    out = nc.dram_tensor("out", (B * C, N), mybir.dt.float32, kind="ExternalOutput").ap()
    build(nc, out=out, **aps)
    res = run(nc, [{f"in_{k}": v for k, v in arrays.items()}], core_ids=[0])
    return res.results[0]["out"].reshape(x.shape)
```

```python
import concourse.bass as bass
from concourse import mybir
from contextlib import ExitStack

B, C, N = 4, 64, 1024
MC = 32
H, D = 8, 64
P = 128
NT = N // P
CW = 512
NC = N // CW
TPC = CW // P
UNITS = B * H
PO = C + 1

ST_RING, MX_RING, P_RING, E_RING = 3, 2, 12, 6
REST_LAG = 3
KEYS_SLOT, KEYS_SLOT3 = 0, 9
LN1_SLOT = 11
LN3_SLOTS = (9, 10, 11)
LN_EPS = 1e-5
ZLOW_LAG = 2
HURRY = 2
LAST_TR_SLOT, LAST_W_SLOT = 6, 9
LAG = 5

HALF_SWEEPS = 5
FULL_SWEEPS = 6
RESIDUAL_LIMIT = 2.0 ** -19

K_IDENT, K_AVG, K_MASK_T, K_MASK_R = 0, 128, 256, 384
CONST_COLS = 512
NEG = -1e30


class Sems:

    def __init__(self, sem, tag):
        self.scores = sem(f"{tag}_scores_in_psum")
        self.probs = sem(f"{tag}_probs_written")
        self.rest_pool = sem(f"{tag}_rest_by_pool")
        self.rest_dve = sem(f"{tag}_rest_by_dve")
        self.values = sem(f"{tag}_values_accumulated")
        self.zcopied = sem(f"{tag}_z_copied")
        self.zlow = sem(f"{tag}_z_low_part")
        self.projected = sem(f"{tag}_chunk_projected")
        self.recip = sem(f"{tag}_recip")
        self.scaled = sem(f"{tag}_chunk_scaled")
        self.added = sem(f"{tag}_chunk_added")
        self.prep = sem(f"{tag}_prep_in_psum")
        self.prep_used = sem(f"{tag}_prep_used")
        self.cast = sem(f"{tag}_high_part_cast")
        self.rowmax = sem(f"{tag}_row_max")
        self.maxrow = sem(f"{tag}_max_row_dma")


class Phase:

    def __init__(self, causal, prep, dve_items):
        self.causal = causal
        self.items = []
        for c in range(NC):
            for j in range(TPC * (c + 1) if causal else NT):
                off = max(0, (j - TPC * c)) * P if causal else 0
                self.items.append((c, j, off, causal and j >= TPC * c))
        self.n = len(self.items)
        self.last = [max(i for i, it in enumerate(self.items) if it[0] == c) for c in range(NC)]
        self.first = [min(i for i, it in enumerate(self.items) if it[0] == c) for c in range(NC)]
        self.maxes = []
        for t in range(NT):
            keys = (t + 1) * P if causal else N
            for part in range((keys + CW - 1) // CW):
                k0 = part * CW
                w = min(CW, keys - k0)
                self.maxes.append((t, part, k0, w, causal and k0 + w == keys))
        self.prep = prep
        self.nprep = prep + len(self.maxes) + 1
        self.dve_items = sorted(dve_items)
        self.pool_items = [i for i in range(self.n) if i not in dve_items]

    def rest_wait(self, s, u, n):
        if n in self.dve_items:
            return s.rest_dve, u * len(self.dve_items) + self.dve_items.index(n) + 1
        return s.rest_pool, u * len(self.pool_items) + self.pool_items.index(n) + 1

    def back(self, u, n, k):
        return (u, n - k) if n >= k else (u - 1, n - k + self.n)


def build(nc, x_cm, x_tm, conv_w, conv_proj, attn_w, ffn, gb, const, out):
    f32, f16, bf16, i32 = mybir.dt.float32, mybir.dt.float16, mybir.dt.bfloat16, mybir.dt.int32
    ALU, ACT, AX = mybir.AluOpType, mybir.ActivationFunctionType, mybir.AxisListType.X
    ds = bass.ds

    CONV = Phase(causal=False, prep=6, dve_items={9, 12})
    ATTN = Phase(causal=True, prep=2, dve_items={5, 7})
    SCALE = float(D) ** -0.5

    ctx = ExitStack()
    with ctx:
        def sb(name, shape, dt=f32):
            return ctx.enter_context(nc.sbuf_tensor(name, shape, dt))

        def sem(name):
            return ctx.enter_context(nc.semaphore(name))

        xc = sb("x_channels", [P, B * N])
        x16 = sb("x_split", [P, B * N], f16)
        tok = sb("tokens", [P, NT * B * C])
        cw = sb("conv_weights", [P, 3 * P])
        cw_hi = sb("conv_weights_high", [P, 3 * P], f16)
        cw_lo = sb("conv_weights_low", [P, 3 * P], f16)
        cproj = sb("conv_projection", [P, PO])
        aw = sb("attn_weights", [P, 4, H // 2, C])
        wo = aw[:, 3]
        ffn_w = sb("ffn_weights", [P, 2, P])
        gbt = sb("gamma_beta", [P, 2])
        cst = sb("constants", [P, CONST_COLS])
        ident16 = sb("identity_fp16", [P, P], f16)
        identbf = sb("identity_bf16", [P, P], bf16)
        masks = sb("causal_masks", [P, 2, P], bf16)
        wqT = sb("wq_pairs_T", [P, H // 2, P])
        wkT = sb("wk_pairs_T", [P, H // 2, P])
        wvT = sb("wv_pairs_T", [P, H // 2, P])
        a_hi = sb("qk_matrix_high", [P, H * P], f16)
        a_lo = sb("qk_matrix_low", [P, H * P], f16)
        proj = sb("attn_projection", [P, H * PO])
        pr_hi = sb("attn_projection_high", [P, H * PO], f16)
        pr_lo = sb("attn_projection_low", [P, H * PO], f16)
        cxs = sb("conv_keys", [P, B * N], f16)
        cxt = sb("conv_values", [P, B * NT * P], f16)
        xs = sb("attn_keys", [P, B * N], f16)
        xt = sb("attn_values", [P, B * NT * P], f16)
        q_hi = [sb(f"queries_high{i}", [P, N], f16) for i in range(2)]
        q_lo = [sb(f"queries_low{i}", [P, N], f16) for i in range(2)]
        e32 = sb("probs32", [P, E_RING, CW])
        p_hi = sb("probs_high", [P, P_RING, CW], f16)
        p_lo = sb("probs_low", [P, P_RING, CW], f16)
        zs = sb("z", [P, NC, CW])
        zs_hi = sb("z_high", [P, NC, CW], f16)
        zs_lo = sb("z_low", [P, NC, CW], f16)
        scaled = sb("scaled_chunks", [P, NC, TPC, C])
        rden = sb("reciprocal_denominators", [P, NC, TPC])
        cmx = [sb(f"conv_partial_max{i}", [P, NT, NC]) for i in range(2)]
        amx = [sb(f"attn_partial_max{i}", [P, NT, NC]) for i in range(2)]
        m8 = [sb(f"row_max{i}", [P, NT]) for i in range(2)]
        mrow = [sb(f"minus_max_rows{i}", [NT, P], f16) for i in range(2)]
        stats = sb("ln_stats", [P, NT, 6])
        mv = sb("ln_mean_var", [P, NT * B, 2])
        mv_one = sb("ln_mean_var_of_one_tile", [P, 2])
        rstd = sb("ln_rstd", [P, NT * B])
        var_eps = sb("ln_var_eps", [P, NT * B])
        nwt = sb("newton_scratch", [P, NT * B])
        xh = sb("ln_out", [P, NT * C])
        xh3 = sb("ln3_tokens", [P, NT * B * C])
        xh3T = sb("ln3_channels", [P, 2 * N])
        t2T = sb("tokens_channels", [P, 2 * N])
        wx = xc[:, 2 * N:4 * N]
        wx16 = sb("wx_fp16", [P, 2 * N], f16)
        v16 = sb("v_fp16", [P, P], f16)
        y16 = [sb(f"y_fp16_{i}", [P, 2, N + 1], f16) for i in range(2)]
        y32 = [sb(f"y_{i}", [P, 2, N + 1]) for i in range(2)]
        zsw = xc[:, 0:2 * N].rearrange("p (k c) -> p k c", k=4)
        bst = sb("bn_stats", [P, 4, 6])
        bmv = sb("bn_mean_var", [P, 2])
        bwk = sb("bn_scratch", [P, 8])
        dmax = sb("last_step_max", [P, 6])
        wait_carrier = sb("wait_carrier", [P, 1])
        sig_table = sb("sigmoid_of_a_constant", [P, 1])
        flag = sb("not_solved", [1, 2], i32)
        zseq = sb("seq_pre_activation", [P, 2])
        diff = zsw.rearrange("p k c -> p (k c)")
        outt = xh3T

        banks = [ctx.enter_context(nc.psum_tensor(f"bank{i}", [P, CW], f32)) for i in range(8)]
        ST, MX, ZT, PJ = banks[0:3], banks[3:5], banks[5:7], banks[7]

        LN_BANKS = [banks[i] for i in (3, 4, 5, 6)]
        WX_BANKS = [banks[i] for i in (3, 4, 0, 1)]
        T2_BANKS = [banks[i] for i in (2, 7, 6, 5)]
        V_BANKS = T2_BANKS

        cs, as_ = Sems(sem, "conv"), Sems(sem, "attn")
        s_x = [sem(f"x_loaded_{b}") for b in range(B)]
        s_cw = sem("conv_weights_loaded")
        s_cproj = sem("conv_projection_loaded")
        s_cws = sem("conv_weights_split")
        s_xh = sem("x_high_parts_by_pool")
        s_x16 = sem("x_split_ready")
        s_tok = sem("tokens_loaded")
        s_w = sem("attn_weights_loaded")
        s_cst = sem("constants_loaded")
        s_ffn = sem("ffn_loaded")
        s_init = sem("dve_constants_ready")
        s_wt = sem("weights_times_d")
        s_am = sem("qk_and_projection_matrices_in_psum")
        s_ahi = sem("qk_matrix_high_ready")
        s_amd = sem("attn_matrices_ready")
        s_chain = sem("dve_chain")
        s_xt = sem("ln_values_ready")
        s_xtp = sem("ln_keys_in_psum")
        s_xs = sem("ln_keys_ready")
        s_ln3 = sem("ln3_statistics")
        s_l3 = sem("ln3_ready")
        s_tr = sem("ln3_transposes_in_psum")
        s_trc = sem("ln3_transposes_copied")
        s_t2 = sem("token_transposes_in_psum")
        s_t2c = sem("token_transposes_copied")
        s_wxp = sem("wx_in_psum")
        s_bn1 = sem("bn_means_local")
        s_bn2 = sem("bn_averages_in_psum")
        s_bn3 = sem("bn_averages_read")
        s_bn5 = sem("bn_affine_ready")
        s_wx = sem("wx_ready")
        s_wx16 = sem("wx16_ready")
        s_v = sem("sweep_products")
        s_z = sem("sweep_pre_activations")
        s_y = sem("sweep_chunks")
        s_df = sem("last_step_chunks")
        s_dm = sem("last_step_max_ready")
        s_dmt = sem("last_step_max_transposed")
        s_flag = sem("flag_ready")
        s_sv = sem("sequential_products")
        s_sz = sem("sequential_pre_activations")
        s_sy = sem("sequential_steps")
        s_out = sem("out_added")
        s_store = sem("out_stored")

        block = ctx.enter_context(nc.Block())
        CHAIN = [0]

        def chunk(y, k):
            return y[:, k // 2, 1 + (k % 2) * CW:1 + (k % 2 + 1) * CW]

        def by_head(t, r):
            return t[:].rearrange("p (g r c) -> p g r c", r=2, c=P)[:, :, r, :]

        def link(ins):
            CHAIN[0] += 1
            ins.then_inc(s_chain, 1)
            nc.vector.wait_ge(s_chain, CHAIN[0])


        def pe_prep_wait(ph, s, u, k):
            g = u * ph.nprep + k
            if not isinstance(g, int) or g >= MX_RING:
                nc.tensor.wait_ge(s.prep_used, g - MX_RING + 1)

        def pe_bank(ph, par, k):
            return MX[(par * ph.nprep + k) % MX_RING]

        def pe_queries(ph, s, u, par, b, h, k):
            pe_prep_wait(ph, s, u, k)
            o = pe_bank(ph, par, k)
            r = xs[:, ds(b * N + k * CW, CW)]
            nc.tensor.matmul(o[:], a_hi[:, ds(h * P, P)], r, start=True, stop=False)
            nc.tensor.matmul(o[:], a_lo[:, ds(h * P, P)], r, start=False, stop=True).then_inc(s.prep, 1)

        def pe_conv_prep(ph, s, u, par, k):
            pe_prep_wait(ph, s, u, k)
            if k == 0:
                nc.tensor.wait_ge(s_x16, u + 1)
            o = pe_bank(ph, par, k)

            def product(dst, stationary, moving):
                for part, (st, mo) in enumerate(zip(stationary, moving)):
                    ins = nc.tensor.matmul(dst, st, mo, start=part == 0, stop=part == 1)
                return ins

            if k < 4:
                cols = slice((k // 2) * P, (k // 2 + 1) * P)
                xk = x16[:, u * N + (k % 2) * CW:u * N + (k % 2 + 1) * CW]
                product(o[:], (cw_hi[:, cols], cw_lo[:, cols]), (xk, xk)).then_inc(s.prep, 1)
            else:
                for t in range(TPC):
                    g = u * N + ((k - 4) * TPC + t) * P
                    last = product(o[:, t * P:(t + 1) * P], (x16[:, g:g + P],) * 2,
                                   (cw_hi[:, 2 * P:3 * P], cw_lo[:, 2 * P:3 * P]))
                last.then_inc(s.prep, 1)

        def pe_rowmax(ph, s, u, par, keys, b, i):
            t, part, k0, w, diag = ph.maxes[i]
            pe_prep_wait(ph, s, u, ph.prep + i)
            o = pe_bank(ph, par, ph.prep + i)
            if ph.causal:
                nc.tensor.wait_ge(s.cast, u * NC + t // TPC + 1)
            else:
                nc.tensor.wait_ge(s.prep_used, u * ph.nprep + 4)
            ins = nc.tensor.matmul(o[:, 0:w], q_hi[par][:, t * P:(t + 1) * P], keys[:, ds(b * N + k0, w)],
                                   start=True, stop=not diag)
            if diag:
                ins = nc.tensor.matmul(o[:, w - P:w], identbf[:], masks[:, 1, :], start=False, stop=True)
            ins.then_inc(s.prep, 1)

        def pe_max_transpose(ph, s, u, par):
            k = ph.nprep - 1
            pe_prep_wait(ph, s, u, k)
            nc.tensor.wait_ge(s.rowmax, u + 1)
            nc.tensor.transpose(pe_bank(ph, par, k)[0:NT, 0:P], m8[par][:], cst[:, K_IDENT:K_IDENT + P]) \
                .then_inc(s.prep, 1)

        def pe_scores(ph, s, u, par, keys, b, n, first_unit):
            c, j, off, diag = ph.items[n]
            g = u * ph.n + n
            if first_unit and not ph.causal and n == 2:
                nc.tensor.wait_ge(s_ahi, 1)
            if not (first_unit and n < ST_RING):
                nc.tensor.wait_ge(s.probs, g - ST_RING + 1)
            if n == 0:
                nc.tensor.wait_ge(s.maxrow, 16 * (u + 1))
                nc.tensor.wait_ge(s.prep_used, (u + 1) * ph.nprep)
            o = ST[n % ST_RING] if ph.n % ST_RING == 0 else ST[(par_base(ph, u) + n) % ST_RING]
            lhs = keys[:, ds(b * N + j * P, P)]
            lo, hi = c * CW + off, (c + 1) * CW
            nc.tensor.matmul(o[:, off:CW], lhs, q_hi[par][:, lo:hi], start=True, stop=False)
            ins = nc.tensor.matmul(o[:, off:CW], lhs, q_lo[par][:, lo:hi], start=False, stop=not diag)
            if diag:
                ins = nc.tensor.matmul(o[:, off:off + P], identbf[:], masks[:, 0, :], start=False, stop=True)
            ins.then_inc(s.scores, 1)

        def par_base(ph, u):
            return u * ph.n if isinstance(u, int) else 0

        def slot(ph, u, n, ring):
            return n % ring if ph.n % ring == 0 else (par_base(ph, u) + n) % ring

        def pe_values(ph, s, u, values, b, n, first_unit):
            c, j, off, _ = ph.items[n]
            if first_unit and not ph.causal and n == 0:
                nc.tensor.wait_ge(s_amd, 1)
            if n == ph.first[c] and not first_unit:
                nc.tensor.wait_ge(s.zcopied, u * NC + c - 1)
                if ph.causal:
                    nc.tensor.wait_ge(s.zlow, u * NC + c - 1)
            nc.tensor.wait_ge(s.probs, u * ph.n + n + 1)
            rs, rv = ph.rest_wait(s, u, n)
            nc.tensor.wait_ge(rs, rv)
            q = slot(ph, u, n, P_RING)
            lhs = values[:, ds((b * NT + j) * P, P)]
            nc.tensor.matmul(ZT[c][:, off:CW], lhs, p_hi[:, q, off:CW], start=(n == ph.first[c]), stop=False)
            nc.tensor.matmul(ZT[c][:, off:CW], lhs, p_lo[:, q, off:CW], start=False,
                             stop=(n == ph.last[c])).then_inc(s.values, 1)

        def pe_project(ph, s, u, pr, c, first_unit):
            nc.tensor.wait_ge(s.zcopied, u * NC + c + 1)
            if not (first_unit and c == 0):
                nc.tensor.wait_ge(s.scaled, u * NC + c)
            if ph.causal:
                nc.tensor.wait_ge(s.zlow, u * NC + c + 1)
            for t in range(TPC):
                cols, dst = slice(t * P, (t + 1) * P), PJ[:, t * PO:(t + 1) * PO]
                if ph.causal:
                    nc.tensor.matmul(dst, zs_hi[:, c, cols], pr[0], start=True, stop=False)
                    nc.tensor.matmul(dst, zs_hi[:, c, cols], pr[1], start=False, stop=False)
                    last = nc.tensor.matmul(dst, zs_lo[:, c, cols], pr[0], start=False, stop=True)
                else:
                    last = nc.tensor.matmul(dst, zs[:, c, cols], pr, start=True, stop=True)
            last.then_inc(s.projected, 1)

        def proj_slot(ph, c):
            return ph.last[c] + LAG + (3 if ph.causal else 2)

        def pe_unit(ph, s, u, par, keys, values, b, pr, prev, nxt, first, keys_slot=None, keys_batch=None,
                    tail=None):
            for n in range(ph.n):
                if tail is not None:
                    tail(n)
                if nxt is not None and n == 0:
                    nxt(n, 0)
                pe_scores(ph, s, u, par, keys, b, n, first)
                if nxt is not None and n > 0:
                    nxt(n, 0)
                if n >= LAG:
                    pe_values(ph, s, u, values, b, n - LAG, first)
                elif prev is not None:
                    pe_values(ph, s, u - 1, prev[0], prev[1], n - LAG + ph.n, prev[3])
                if nxt is not None:
                    nxt(n, 1)
                if n == keys_slot:
                    pe_xs_transposes(keys_batch)
                if keys_slot is not None and n == min(keys_slot + 2, ph.n - 1):
                    nc.tensor.wait_ge(s_xs, keys_batch + 1)
                for c in range(NC):
                    if n == proj_slot(ph, c) - (HURRY if tail is not None else 0):
                        pe_project(ph, s, u, pr, c, first)
                    if prev is not None and n == proj_slot(ph, c) - ph.n:
                        pe_project(ph, s, u - 1, prev[2], c, prev[3])

        def pe_drain(ph, s, u, values, b, pr):
            for n in range(ph.n, ph.n + LAG):
                pe_values(ph, s, u, values, b, n - LAG, False)
            pe_project(ph, s, u, pr, NC - 1, False)

        def a_slot_steps(ph, n):
            if ph.causal:
                table = {0: range(0, 2)}
                for i in range(6):
                    table[1 + i] = range(2 + 2 * i, 4 + 2 * i)
                table[9] = range(14, 15)
            else:
                table = {0: range(0, 2), 1: range(2, 4), 2: range(4, 6)}
                for i in range(8):
                    table[3 + i] = range(6 + 2 * i, 8 + 2 * i)
                table[11] = range(22, 23)
            return table.get(n, range(0))

        def half_of(steps, n, half):
            if n == 0:
                return [] if half else list(steps)
            return list(steps)[1:] if half else list(steps)[:1]

        def pe_a_step(ph, s, u, par, keys, b, h, k):
            if k < ph.prep:
                if ph.causal:
                    if h is not None:
                        pe_queries(ph, s, u, par, b, h, k)
                else:
                    pe_conv_prep(ph, s, u, par, k)
            elif k < ph.nprep - 1:
                pe_rowmax(ph, s, u, par, keys, b, k - ph.prep)
            else:
                pe_max_transpose(ph, s, u, par)

        def pr_of(h):
            return pr_hi[:, ds(h * PO, PO)], pr_lo[:, ds(h * PO, PO)]

        def pe_attn_unit(u, par, last=False, first=False):
            b, h = u // H, u % H
            v = u + 1
            bn, hn = v // H, v % H
            nxt = None if last else (lambda n, half: [pe_a_step(ATTN, as_, v, 1 - par, xs, bn, hn, k)
                                                      for k in half_of(a_slot_steps(ATTN, n), n, half)])
            prev = None
            if not first:
                w = u - 1
                prev = (xt, w // H, pr_of(w % H), isinstance(w, int) and w == 0)
            pe_unit(ATTN, as_, u, par, xs, xt, b, pr_of(h), prev, nxt, first,
                    KEYS_SLOT3 if first else None, B - 1, pe_early_tail if last else None)

        def pe_transposes(dst, src, k):
            for t in range(TPC):
                g = ((k % 2) * TPC + t) * B * C + (k // 2) * P
                last = nc.tensor.transpose(dst[:, t * P:(t + 1) * P], src[:, g:g + P], cst[:, K_IDENT:K_IDENT + P])
            return last

        def pe_ln_transposes(k):
            nc.tensor.wait_ge(s_l3, k + 1)
            pe_transposes(LN_BANKS[k], xh3, k).then_inc(s_tr, 1)

        def pe_w(k):
            nc.tensor.wait_ge(s_trc, k + 1)
            nc.tensor.matmul(WX_BANKS[k][:], ffn_w[:, 0, :], xh3T[:, k * CW:(k + 1) * CW],
                             start=True, stop=True).then_inc(s_wxp, 1)

        def pe_early_tail(n):
            if n in (LAST_TR_SLOT, LAST_TR_SLOT + 1):
                pe_ln_transposes(n - LAST_TR_SLOT)
            if n == LAST_W_SLOT:
                nc.tensor.wait_ge(s_ffn, 32)
            if n in (LAST_W_SLOT, LAST_W_SLOT + 1):
                pe_w(n - LAST_W_SLOT)

        def pe_xs_transposes(b):
            pe = nc.tensor
            pe.wait_ge(s_xt, b + 1)
            pe.wait_ge(cs.scaled, (b + 2) * NC - 1 if b < B - 2 else B * NC)
            if b:
                pe.wait_ge(s_xs, b)
            for t in range(NT):
                last = nc.tensor.transpose(PT16[:, t * P:(t + 1) * P], xt[:, (b * NT + t) * P:(b * NT + t + 1) * P],
                                           ident16[:])
            last.then_inc(s_xtp, 1)

        PT16 = PJ[:].bitcast(f16)
        mv4 = mv[:].rearrange("p (t b) s -> p t b s", b=B)
        tok3 = tok[:].rearrange("p (t m) -> p t m", t=NT)

        @block.tensor
        def _(pe):
            pe.wait_ge(s_cws, 1)
            pe.wait_ge(s_x16, 1)
            for k in range(CONV.prep):
                pe_a_step(CONV, cs, 0, 0, cxs, 0, None, k)
            pe.wait_ge(s_cst, 16)
            pe.wait_ge(s_w, 16)
            pe.wait_ge(s_wt, 3)
            for k in range(CONV.prep, CONV.nprep):
                pe_a_step(CONV, cs, 0, 0, cxs, 0, None, k)
                h = k - CONV.prep
                r, pair = C * (h % 2), (h % H) // 2
                if h < H:
                    nc.tensor.matmul(banks[5 + h % 2][:, pair * P:(pair + 1) * P], wqT[r:r + C, pair, :],
                                     wkT[r:r + C, pair, :], start=True, stop=True)
                elif h < 2 * H:
                    ins = nc.tensor.matmul(banks[(7, 2)[h % 2]][:, pair * C:(pair + 1) * C], wvT[r:r + C, pair, :],
                                           wo[r:r + C, pair, :], start=True, stop=True)
                    if h == 2 * H - 1:
                        ins.then_inc(s_am, 1)
            pe.wait_ge(s_init, 1)
            pe.wait_ge(s_cproj, 16)
            for u in range(B):
                if u < B - 1:
                    def nxt(n, half, v=u + 1):
                        for k in half_of(a_slot_steps(CONV, n), n, half):
                            pe_a_step(CONV, cs, v, v % 2, cxs, v, None, k)
                else:
                    def nxt(n, half):
                        for k in half_of(a_slot_steps(ATTN, n), n, half):
                            pe_a_step(ATTN, as_, 0, 0, xs, 0, 0, k)
                prev = (cxt, u - 1, cproj[:], u - 1 == 0) if u else None
                pe_unit(CONV, cs, u, u % 2, cxs, cxt, u, cproj[:], prev, nxt, u == 0,
                        KEYS_SLOT if u >= 2 else None, u - 2)
            pe_drain(CONV, cs, B - 1, cxt, B - 1, cproj[:])
            pe_xs_transposes(2)

            pe_attn_unit(0, 0, first=True)
            with pe.Fori(0, (UNITS - 2) // 2) as i:
                pe_attn_unit(1 + 2 * i, 1)
                pe_attn_unit(2 + 2 * i, 0)
            pe_attn_unit(UNITS - 1, 1, last=True)
            pe_drain(ATTN, as_, UNITS - 1, xt, B - 1, pr_of(H - 1))

            pe_ln_transposes(2)
            pe_transposes(T2_BANKS[0], tok, 0).then_inc(s_t2, 1)
            pe_w(2)
            pe_ln_transposes(3)
            pe_w(3)
            pe.wait_ge(s_bn1, 1)
            nc.tensor.matmul(T2_BANKS[3][:, 0:2], cst[:, K_AVG:K_AVG + P], bmv[:], start=True, stop=True) \
                .then_inc(s_bn2, 1)
            for k in range(1, 4):
                if k == 3:
                    pe.wait_ge(s_bn3, 1)
                pe_transposes(T2_BANKS[k], tok, k).then_inc(s_t2, 1)

            for w in range(HALF_SWEEPS):
                for k in range(4):
                    if w == 0:
                        pe.wait_ge(s_wx16, k + 1)
                        pe.wait_ge(s_t2c, k + 1)
                    pe.wait_ge(s_y, 4 * w + k + 1)
                    yp = y16[w % 2][:, k // 2, (k % 2) * CW:(k % 2) * CW + CW]
                    nc.tensor.matmul(V_BANKS[k][:], ident16[:], wx16[:, k * CW:(k + 1) * CW], start=True, stop=False)
                    nc.tensor.matmul(V_BANKS[k][:], v16[:], yp, start=False, stop=True).then_inc(s_v, 1)
            for w in range(FULL_SWEEPS):
                for k in range(4):
                    pe.wait_ge(s_y, 4 * (HALF_SWEEPS + w) + k + 1)
                    yp = y32[w % 2][:, k // 2, (k % 2) * CW:(k % 2) * CW + CW]
                    nc.tensor.matmul(V_BANKS[k][:], ffn_w[:, 1, :], yp, start=True, stop=True).then_inc(s_v, 1)
            pe.wait_ge(s_dm, 1)
            nc.tensor.transpose(banks[4][0:1, 0:P], dmax[:, 4:5], cst[:, K_IDENT:K_IDENT + P]).then_inc(s_dmt, 1)
            pe.wait_ge(s_flag, 1)
            f = pe.value_load(flag[0:1, 0:1], min_val=0, max_val=1)
            yl = y32[FULL_SWEEPS % 2]
            with pe.If(f > 0):
                with pe.Fori(0, N) as t:
                    pe.wait_ge(s_sy, t + 1)
                    nc.tensor.matmul(banks[0][:, 0:2], ffn_w[:, 1, :], yl[:, :, ds(t, 1)].rearrange("p a b -> p (a b)"),
                                     start=True, stop=True).then_inc(s_sv, 1)

        def act_item(ph, s, u, n, first_unit, scale):
            c, j, off, _ = ph.items[n]
            g = u * ph.n + n
            nc.scalar.wait_ge(s.scores, g + 1)
            if not (first_unit and n < E_RING):
                rs, rv = ph.rest_wait(s, *ph.back(u, n, E_RING))
                nc.scalar.wait_ge(rs, rv)
            if not (first_unit and n < P_RING):
                nc.scalar.wait_ge(s.values, g - P_RING + 1)
            o = ST[slot(ph, u, n, ST_RING)]
            e, q = slot(ph, u, n, E_RING), slot(ph, u, n, P_RING)
            nc.scalar.activation(e32[:, e, off:CW], o[:, off:CW], ACT.Exp, scale=scale)
            nc.scalar.activation(p_hi[:, q, off:CW], o[:, off:CW], ACT.Exp, scale=scale).then_inc(s.probs, 1)

        def act_cast(ph, s, u, par, k):
            nc.scalar.wait_ge(s.prep, u * ph.nprep + k + 1)
            src = MX[(par * ph.nprep + k) % MX_RING]
            if ph.causal:
                dst = q_hi[par][:, k * CW:(k + 1) * CW]
            elif k < 2:
                dst = cxs[:, u * N + k * CW:u * N + (k + 1) * CW]
            elif k < 4:
                dst = q_hi[par][:, (k - 2) * CW:(k - 1) * CW]
            else:
                dst = cxt[:, (u * NT + (k - 4) * TPC) * P:(u * NT + (k - 3) * TPC) * P]
            if not ph.causal and k < 2:
                nc.scalar.activation(dst, src[:], ACT.Identity, bias=cst[:, K_IDENT:K_IDENT + 1]).then_inc(s.cast, 1)
            else:
                nc.scalar.activation(dst, src[:], ACT.Copy).then_inc(s.cast, 1)

        def act_zcopy(ph, s, u, c, first_unit):
            nc.scalar.wait_ge(s.values, u * ph.n + ph.last[c] + 1)
            nc.scalar.activation(zs_hi[:, c, :] if ph.causal else zs[:, c, :], ZT[c][:], ACT.Copy).then_inc(s.zcopied, 1)

        def zslot(ph, c):
            return ph.last[c] + LAG + -1

        def act_xs_copy(b):
            nc.scalar.wait_ge(s_xtp, b + 1)
            nc.scalar.activation(xs[:, b * N:(b + 1) * N], PT16, ACT.Copy).then_inc(s_xs, 1)

        def act_unit(ph, s, u, par, first, prev_first, has_prev, nxt, scale, keys_slot=None, keys_batch=None,
                     first_attn=False, last=False):
            for n in range(ph.n):
                if last and n in (LAST_TR_SLOT + 1, LAST_TR_SLOT + 2):
                    act_ln_copy(n - LAST_TR_SLOT - 1)
                if nxt:
                    for k in a_slot_steps(ph, n):
                        if k < ph.prep:
                            act_cast(ph, s, u + 1, 1 - par, k)
                if first_attn:
                    for k in a_slot_steps(ATTN, n):
                        if k < ATTN.prep:
                            act_cast(ATTN, as_, 0, 0, k)
                act_item(ph, s, u, n, first, scale)
                if n == keys_slot:
                    act_xs_copy(keys_batch)
                for c in range(NC):
                    if n == zslot(ph, c):
                        act_zcopy(ph, s, u, c, first)
                    if has_prev and n == zslot(ph, c) - ph.n:
                        act_zcopy(ph, s, u - 1, c, prev_first)

        def act_ln_copy(k):
            nc.scalar.wait_ge(s_tr, k + 1)
            nc.scalar.activation(xh3T[:, k * CW:(k + 1) * CW], LN_BANKS[k][:], ACT.Copy).then_inc(s_trc, 1)

        @block.scalar
        def _(act):
            act.dma_start(xc[C:P, 0:N], x_cm[0]).then_inc(s_x[0], 16)
            act.dma_start(cst[:], const).then_inc(s_cst, 16)
            act.dma_start(aw[:].rearrange("p w g c -> p (w g c)"), attn_w).then_inc(s_w, 16)
            act.wait_ge(s_cst, 16)
            for k in range(CONV.prep):
                act_cast(CONV, cs, 0, 0, k)
            act.wait_ge(s_am, 1)
            for r in range(2):
                nc.scalar.activation(by_head(a_hi, r), banks[5 + r][:].rearrange("p (g c) -> p g c", c=P), ACT.Copy)
                ins = nc.scalar.activation(proj[:].rearrange("p (g r c) -> p g r c", r=2, c=PO)[:, :, r, 0:C],
                                           banks[(7, 2)[r]][:, 0:H // 2 * C].rearrange("p (g c) -> p g c", c=C), ACT.Copy)
            ins.then_inc(s_ahi, 1)
            for u in range(B):
                act_unit(CONV, cs, u, u % 2, u == 0, u == 1, u > 0, u < B - 1, 1.0,
                         KEYS_SLOT if u >= 2 else None, u - 2, first_attn=u == B - 1)
            act_zcopy(CONV, cs, B - 1, NC - 1, False)
            act_xs_copy(2)
            act.wait_ge(cs.values, B * CONV.n)
            act_unit(ATTN, as_, 0, 0, True, False, False, True, SCALE, KEYS_SLOT3, B - 1)
            with act.Fori(0, (UNITS - 2) // 2) as i:
                act_unit(ATTN, as_, 1 + 2 * i, 1, False, True, True, True, SCALE)
                act_unit(ATTN, as_, 2 + 2 * i, 0, False, False, True, True, SCALE)
            act_unit(ATTN, as_, UNITS - 1, 1, False, False, True, False, SCALE, last=True)
            act_zcopy(ATTN, as_, UNITS - 1, NC - 1, False)
            nc.scalar.activation(sig_table[:], cst[:, 0:1], ACT.Sigmoid)
            for k in range(2, 4):
                act_ln_copy(k)
            for k in range(4):
                act.wait_ge(s_t2, k + 1)
                nc.scalar.activation(t2T[:, k * CW:(k + 1) * CW], T2_BANKS[k][:], ACT.Copy).then_inc(s_t2c, 1)
            act.wait_ge(s_bn5, 1)
            for k in range(4):
                nc.scalar.activation(y16[0][:, k // 2, 1 + (k % 2) * CW:1 + (k % 2) * CW + CW],
                                     WX_BANKS[k][:], ACT.Sigmoid, scale=bwk[:, 5:6], bias=bwk[:, 6:7]).then_inc(s_y, 1)
            for w in range(HALF_SWEEPS):
                dst = y16[(w + 1) % 2] if w < HALF_SWEEPS - 1 else y32[0]
                for k in range(4):
                    act.wait_ge(s_v, 4 * w + k + 1)
                    if w >= 1:
                        act.wait_ge(s_v, min(4 * w + k + 1, 4 * (w - 1) + k + 2))
                    nc.scalar.activation(dst[:, k // 2, 1 + (k % 2) * CW:1 + (k % 2) * CW + CW],
                                         V_BANKS[k][:], ACT.Sigmoid).then_inc(s_y, 1)
            for w in range(FULL_SWEEPS):
                dst = y32[(w + 1) % 2]
                for k in range(4):
                    act.wait_ge(s_z, 4 * w + k + 1)
                    nc.scalar.activation(dst[:, k // 2, 1 + (k % 2) * CW:1 + (k % 2) * CW + CW],
                                         zsw[:, k, :], ACT.Sigmoid).then_inc(s_y, 1)
            act.wait_ge(s_flag, 1)
            f = act.value_load(flag[0:1, 0:1], min_val=0, max_val=1)
            yl = y32[FULL_SWEEPS % 2]
            with act.If(f > 0):
                with act.Fori(0, N) as t:
                    act.wait_ge(s_sz, t + 1)
                    nc.scalar.activation(yl[:, :, ds(t + 1, 1)].rearrange("p a b -> p (a b)"), zseq[:],
                                         ACT.Sigmoid).then_inc(s_sy, 1)

        def rest_item(eng, ph, s, u, n, first_unit):
            off = ph.items[n][2]
            g = u * ph.n + n
            eng.wait_ge(s.probs, g + 1)
            if not (first_unit and n < P_RING):
                eng.wait_ge(s.values, g - P_RING + 1)
            e, q = slot(ph, u, n, E_RING), slot(ph, u, n, P_RING)
            rs, _ = ph.rest_wait(s, u, n)
            eng.tensor_tensor(out=p_lo[:, q, off:CW], in0=e32[:, e, off:CW], in1=p_hi[:, q, off:CW],
                              op=ALU.subtract).then_inc(rs, 1)

        def dve_a_step(ph, s, u, par, k):
            dve = nc.vector
            src = MX[(par * ph.nprep + k) % MX_RING]
            dve.wait_ge(s.prep, u * ph.nprep + k + 1)
            mxs = (amx if ph.causal else cmx)[par]
            if k < ph.prep:
                dve.wait_ge(s.cast, u * ph.prep + k + 1)
                if ph.causal:
                    a = q_hi[par][:, k * CW:(k + 1) * CW]
                    nc.vector.tensor_tensor(out=q_lo[par][:, k * CW:(k + 1) * CW], in0=src[:], in1=a,
                                            op=ALU.subtract).then_inc(s.prep_used, 1)
                elif k < 2:
                    a = cxs[64:96, u * N + k * CW:u * N + (k + 1) * CW]
                    nc.vector.tensor_tensor(out=a, in0=src[64:96, :], in1=a, op=ALU.subtract).then_inc(s.prep_used, 1)
                elif k < 4:
                    a = q_hi[par][:, (k - 2) * CW:(k - 1) * CW]
                    nc.vector.tensor_tensor(out=q_lo[par][:, (k - 2) * CW:(k - 1) * CW], in0=src[:], in1=a,
                                            op=ALU.subtract).then_inc(s.prep_used, 1)
                else:
                    g = (u * NT + (k - 4) * TPC) * P
                    a = cxt[:, g:g + CW].rearrange("p (t c) -> p t c", t=TPC)
                    nc.vector.memset(a[:, :, 0:1], 1.0)
                    nc.vector.tensor_tensor(out=a[:, :, 64:96], in0=src[:].rearrange("p (t c) -> p t c", t=TPC)[:, :, 64:96],
                                            in1=a[:, :, 64:96], op=ALU.subtract).then_inc(s.prep_used, 1)
            elif k < ph.nprep - 1:
                t, part, k0, w, diag = ph.maxes[k - ph.prep]
                nc.vector.reduce_max(mxs[:, t, part:part + 1], src[:, 0:w], AX).then_inc(s.prep_used, 1)
            else:
                nc.vector.tensor_scalar(mrow[par][:], src[0:NT, 0:P], -1.0, None, ALU.mult).then_inc(s.prep_used, 1)

        def dve_rowmax(ph, s, u, par):
            mxs = (amx if ph.causal else cmx)[par]
            nc.vector.wait_ge(s.prep_used, (u + 1) * ph.nprep - 1)
            nc.vector.reduce_max(m8[par][:], mxs[:], AX).then_inc(s.rowmax, 1)

        def dve_zlow(s, u, c):
            nc.vector.wait_ge(s.zcopied, u * NC + c + 1)
            nc.vector.tensor_tensor(out=zs_lo[:, c, :], in0=ZT[c][:], in1=zs_hi[:, c, :],
                                    op=ALU.subtract).then_inc(s.zlow, 1)

        def dve_scale(ph, s, u, c, first_unit):
            dve = nc.vector
            dve.wait_ge(s.projected, u * NC + c + 1)
            pj = PJ[:, 0:TPC * PO].rearrange("p (t c) -> p t c", c=PO)
            nc.vector.reciprocal(rden[:, c, :], pj[:, :, C:PO].rearrange("p t c -> p (t c)")).then_inc(s.recip, 1)
            if not first_unit:
                dve.wait_ge(s.added, u * NC + c - 1)
            dve.wait_ge(s.recip, u * NC + c + 1)
            nc.vector.tensor_tensor(out=scaled[:, c, :, :], in0=pj[:, :, 0:C],
                                    in1=rden[:, c, :].unsqueeze(2).to_broadcast([P, TPC, C]),
                                    op=ALU.mult).then_inc(s.scaled, 1)

        def pool_add(ph, s, u, b, c, first_unit):
            nc.gpsimd.wait_ge(s.scaled, u * NC + c + 1)
            if not (first_unit and c == 0):
                nc.gpsimd.wait_ge(s.added, u * NC + c)
            dst = tok3[:, c * TPC:(c + 1) * TPC, ds(b * C, C)]
            nc.gpsimd.tensor_tensor(out=dst, in0=scaled[:, c, :, :], in1=dst, op=ALU.add).then_inc(s.added, 1)

        def dve_rest_drain(ph):
            return [n for n in range(ph.n - REST_LAG, ph.n) if n in ph.dve_items]

        def dve_drain(ph, s, u):
            for n in dve_rest_drain(ph):
                rest_item(nc.vector, ph, s, u, n, False)
            dve_scale(ph, s, u, NC - 1, False)

        def rowmax_slot(ph):
            return 6 if ph.causal else 10

        def add_slot(ph, c):
            return ph.last[c] + LAG + (3 if ph.causal else 2)

        def dve_unit(ph, s, u, par, b, bprev, first, prev_first, has_prev, nxt, ln1=None, first_attn=False,
                     last=False):
            ahead = (ATTN, as_, 0, 0) if first_attn else (ph, s, u + 1, 1 - par) if nxt else None
            ln3_slots = (0, 1, 2) if last else LN3_SLOTS

            def stage_a(n):
                if ahead is None:
                    return
                for k in a_slot_steps(ahead[0], n):
                    dve_a_step(*ahead, k)
                if n == rowmax_slot(ahead[0]):
                    dve_rowmax(*ahead)

            def rest(n):
                if n - REST_LAG in ph.dve_items:
                    rest_item(nc.vector, ph, s, u, n - REST_LAG, first)
                if has_prev and n - REST_LAG + ph.n in ph.dve_items:
                    rest_item(nc.vector, ph, s, u - 1, n - REST_LAG + ph.n, prev_first)

            def zlow(n):
                for c in range(NC):
                    if ph.causal and n == zslot(ph, c) + ZLOW_LAG:
                        dve_zlow(s, u, c)
                    if ph.causal and has_prev and n == zslot(ph, c) + ZLOW_LAG - ph.n:
                        dve_zlow(s, u - 1, c)

            def scale(n):
                for c in range(NC):
                    if n == add_slot(ph, c) - (HURRY if last else 0):
                        dve_scale(ph, s, u, c, first)
                    if has_prev and n == add_slot(ph, c) - ph.n:
                        dve_scale(ph, s, u - 1, c, prev_first)

            def norms(n):
                if ln1 is not None:
                    per_slot = 1 if ph.causal else 2
                    for step in range(LN_STEPS):
                        if n == ln1[1] + step // per_slot:
                            dve_ln1(ln1[0], step)
                if ph.causal and n in ln3_slots:
                    dve_ln3_stats(u, ln3_slots.index(n), last)

            for n in range(ph.n):
                if last:
                    dve_early_tail(n)
                if ph.causal and n == ln3_slots[1]:
                    nc.vector.wait_ge(s_ln3, 3 * u + 1)
                    nc.vector.memset(wait_carrier[:], 0.0)
                stage_a(n)
                rest(n)
                zlow(n)
                scale(n)
                norms(n)

        def dve_rsqrt_start(r, v):
            link(nc.vector.tensor_scalar(r.bitcast(i32), v.bitcast(i32), -0.5, 1597463007.0, ALU.mult, ALU.add))

        def dve_newton(r, v, w):
            link(nc.vector.tensor_tensor(out=w, in0=r, in1=v, op=ALU.mult))
            link(nc.vector.scalar_tensor_tensor(out=w, in0=w, scalar=-0.5, in1=r, op0=ALU.mult, op1=ALU.mult))
            link(nc.vector.scalar_tensor_tensor(out=r, in0=w, scalar=1.5, in1=r, op0=ALU.add, op1=ALU.mult))

        def dve_rsqrt(r, v, w):
            dve_rsqrt_start(r, v)
            for _ in range(3):
                dve_newton(r, v, w)

        LN_STEPS = 8

        def dve_ln1(b, step):
            x3 = xh[:].rearrange("p (t c) -> p t c", c=C)
            v3 = xt[:, b * NT * P:(b + 1) * NT * P].rearrange("p (t c) -> p t c", c=P)
            if step == 0:
                nc.vector.wait_ge(cs.added, (b + 1) * NC)
                for t in range(NT):
                    ins = nc.vector.bn_stats(stats[:, t, :], tok[:, (t * B + b) * C:(t * B + b + 1) * C])
                link(ins)
            elif step == 1:
                for t in range(NT):
                    ins = nc.vector.bn_aggr(mv[:, t, :], stats[:, t, :])
                link(ins)
                link(nc.vector.tensor_scalar_add(var_eps[:, 0:NT], mv[:, 0:NT, 1:2].rearrange("p t c -> p (t c)"), LN_EPS))
            elif step < 5:
                if step == 2:
                    dve_rsqrt_start(rstd[:, 0:NT], var_eps[:, 0:NT])
                dve_newton(rstd[:, 0:NT], var_eps[:, 0:NT], nwt[:, 0:NT])
            elif step == 5:
                link(nc.vector.tensor_tensor(out=x3, in0=tok3[:, :, b * C:(b + 1) * C],
                                             in1=mv[:, 0:NT, 0:1].to_broadcast([P, NT, C]), op=ALU.subtract))
                link(nc.vector.tensor_tensor(out=x3, in0=x3, in1=rstd[:, 0:NT].unsqueeze(2).to_broadcast([P, NT, C]),
                                             op=ALU.mult))
            elif step == 6:
                link(nc.vector.tensor_copy(v3[:, :, 0:C], x3))
            else:
                link(nc.vector.tensor_tensor(out=v3[:, :, C:P], in0=x3, in1=v3[:, :, 0:C], op=ALU.subtract))
                nc.vector.memset(v3[:, :, 0:1], 1.0)
                nc.vector.memset(v3[:, :, C:C + 1], 0.0).then_inc(s_xt, 1)

        def dve_ln3_stats(u, part, last):
            b, t = (u // H + B - 1) % B, u % NT
            if part == 0:
                if last:
                    nc.vector.wait_ge(as_.added, (B - 1) * H * NC)
                elif not (isinstance(u, int) and u == 0):
                    nc.vector.wait_ge(as_.added, u * NC)
                nc.vector.bn_stats(stats[:, 0, :], tok[:, ds(t * (B * C) + b * C, C)]).then_inc(s_ln3, 1)
            elif part == 1:
                nc.vector.bn_aggr(mv_one[:], stats[:, 0, :]).then_inc(s_ln3, 1)
            else:
                nc.vector.wait_ge(s_ln3, 3 * u + 2)
                nc.vector.tensor_copy(mv[:, ds(t * B + b, 1), :].rearrange("p a c -> p (a c)"),
                                      mv_one[:]).then_inc(s_ln3, 1)

        def last_stats(c):
            nc.vector.wait_ge(as_.added, (UNITS - 1) * NC + c + 1)
            for t in range(c * TPC, (c + 1) * TPC):
                ins = nc.vector.bn_stats(stats[:, t, :], tok[:, (t * B + B - 1) * C:(t + 1) * B * C])
            link(ins)
            for t in range(c * TPC, (c + 1) * TPC):
                ins = nc.vector.bn_aggr(mv[:, t * B + B - 1, :], stats[:, t, :])
            return ins

        def ln3_rstd(b0, b1, t0=0, t1=NT):
            v, r, w = (x[:].rearrange("p (t b) -> p t b", b=B)[:, t0:t1, b0:b1] for x in (var_eps, rstd, nwt))
            link(nc.vector.tensor_scalar_add(v, mv4[:, t0:t1, b0:b1, 1], LN_EPS))
            dve_rsqrt(r, v, w)

        def ln3_apply(k, b0, b1):
            tiles = slice(k * TPC, (k + 1) * TPC)
            shape = [P, TPC, b1 - b0, C]
            x, y = (a[:].rearrange("p (t b c) -> p t b c", b=B, c=C)[:, tiles, b0:b1, :] for a in (tok, xh3))
            mean = mv4[:, tiles, b0:b1, 0:1].to_broadcast(shape)
            scale = rstd[:].rearrange("p (t b) -> p t b", b=B)[:, tiles, b0:b1].unsqueeze(3).to_broadcast(shape)
            link(nc.vector.tensor_tensor(out=y, in0=x, in1=mean, op=ALU.subtract))
            return nc.vector.tensor_tensor(out=y, in0=y, in1=scale, op=ALU.mult)

        def dve_early_tail(n):
            if n == 3:
                nc.vector.wait_ge(s_ln3, 3 * UNITS)
                ln3_rstd(0, B - 1)
            elif n in (4, 5):
                ln3_apply(n - 4, 0, 2).then_inc(s_l3, 1)
            elif n == 6:
                ln3_apply(0, 2, 3)
            elif n == 7:
                ln3_apply(1, 2, 3)
            elif n == ATTN.n - 1:
                for k in range(2):
                    bn_partial(k)

        def bn_partial(k):
            nc.vector.wait_ge(s_wxp, k + 1)
            return nc.vector.bn_stats(bst[:, k, :], WX_BANKS[k][:])

        @block.vector
        def _(dve):
            dve.wait_ge(s_cw, 16)
            link(nc.vector.tensor_copy(cw_hi[:], cw[:]))
            nc.vector.tensor_tensor(out=cw_lo[:], in0=cw[:], in1=cw_hi[:], op=ALU.subtract).then_inc(s_cws, 1)
            dve.wait_ge(s_x[0], 32)
            link(nc.vector.tensor_copy(x16[:, 0:N], xc[:, 0:N]))
            nc.vector.tensor_tensor(out=x16[C:P, 0:N], in0=xc[C:P, 0:N], in1=x16[C:P, 0:N],
                                    op=ALU.subtract).then_inc(s_x16, 1)
            dve.wait_ge(s_cst, 16)
            nc.vector.tensor_copy(ident16[:], cst[:, K_IDENT:K_IDENT + P])
            nc.vector.tensor_copy(identbf[:], cst[:, K_IDENT:K_IDENT + P])
            nc.vector.tensor_copy(masks[:].rearrange("p a c -> p (a c)"), cst[:, K_MASK_T:K_MASK_T + 2 * P]) \
                .then_inc(s_init, 1)
            for i in range(2):
                nc.vector.memset(amx[i][:], -3e38)
                nc.vector.memset(y16[i][:, :, 0:1], 0.0)
                nc.vector.memset(y32[i][:, :, 0:1], 0.0)
            pj3 = proj[:].rearrange("p (h c) -> p h c", c=PO)
            link(nc.vector.memset(pj3[:, :, C:PO], 0.0))
            link(nc.vector.memset(pj3[0:1, :, C:PO], 1.0))
            dve.wait_ge(s_tok, 16)
            for k in range(CONV.nprep):
                if k == CONV.nprep - 1:
                    dve_rowmax(CONV, cs, 0, 0)
                dve_a_step(CONV, cs, 0, 0, k)
            dve.wait_ge(s_ahi, 1)
            for r in range(2):
                ins = nc.vector.tensor_tensor(out=by_head(a_lo, r), in0=banks[5 + r][:].rearrange("p (g c) -> p g c", c=P),
                                              in1=by_head(a_hi, r), op=ALU.subtract)
            ins.then_inc(s_amd, 1)
            link(nc.vector.tensor_copy(pr_hi[:], proj[:]))
            nc.vector.tensor_tensor(out=pr_lo[:], in0=proj[:], in1=pr_hi[:], op=ALU.subtract)
            for u in range(B):
                dve_unit(CONV, cs, u, u % 2, u, u - 1, u == 0, u == 1, u > 0, u < B - 1,
                         ln1=(u - 1, LN1_SLOT) if u else None, first_attn=u == B - 1)
            dve_drain(CONV, cs, B - 1)
            dve_unit(ATTN, as_, 0, 0, 0, 0, True, False, False, True, ln1=(B - 1, 0))
            with dve.Fori(0, (UNITS - 2) // 2) as i:
                dve_unit(ATTN, as_, 1 + 2 * i, 1, (1 + 2 * i) // H, (2 * i) // H, False, True, True, True)
                dve_unit(ATTN, as_, 2 + 2 * i, 0, (2 + 2 * i) // H, (1 + 2 * i) // H, False, False, True, True)
            dve_unit(ATTN, as_, UNITS - 1, 1, B - 1, B - 1, False, False, True, False, last=True)
            for n in dve_rest_drain(ATTN):
                rest_item(nc.vector, ATTN, as_, UNITS - 1, n, False)
            for c in range(NC):
                if c == 0:
                    dve_zlow(as_, UNITS - 1, NC - 1)
                link(last_stats(c))
                ln3_rstd(B - 1, B, c * TPC, (c + 1) * TPC)
                if c == 0:
                    dve_scale(ATTN, as_, UNITS - 1, NC - 1, False)
                ln3_apply(c, B - 1, B).then_inc(s_l3, 1)
            nc.vector.tensor_copy(v16[:], ffn_w[:, 1, :])
            bn_partial(2)
            link(bn_partial(3))
            nc.vector.bn_aggr(bmv[:], bst[:].rearrange("p k c -> p (k c)")).then_inc(s_bn1, 1)
            dve.wait_ge(s_bn1, 1)
            dve.wait_ge(s_bn2, 1)
            avg = T2_BANKS[3]
            nc.vector.tensor_copy(bwk[:, 0:1], avg[:, 0:1])
            nc.vector.tensor_tensor(out=bwk[:, 1:2], in0=bmv[:, 0:1], in1=avg[:, 0:1], op=ALU.subtract)
            nc.vector.tensor_scalar_add(bwk[:, 2:3], avg[:, 1:2], 1e-5).then_inc(s_bn3, 1)
            dve.wait_ge(s_bn3, 1)
            link(nc.vector.scalar_tensor_tensor(out=bwk[:, 3:4], in0=bwk[:, 1:2], scalar=bwk[:, 1:2], in1=bwk[:, 2:3],
                                                op0=ALU.mult, op1=ALU.add))
            r, t = bwk[:, 4:5], bwk[:, 7:8]
            nc.vector.tensor_scalar(bwk[:, 2:3], bwk[:, 3:4], -0.5, None, ALU.mult)
            dve_rsqrt_start(r, bwk[:, 3:4])
            for _ in range(3):
                link(nc.vector.scalar_tensor_tensor(out=t, in0=r, scalar=r, in1=bwk[:, 2:3],
                                                    op0=ALU.mult, op1=ALU.mult))
                link(nc.vector.scalar_tensor_tensor(out=r, in0=t, scalar=1.5, in1=r, op0=ALU.add, op1=ALU.mult))
            link(nc.vector.tensor_tensor(out=bwk[:, 5:6], in0=bwk[:, 4:5], in1=gbt[:, 0:1], op=ALU.mult))
            link(nc.vector.tensor_tensor(out=bwk[:, 7:8], in0=bwk[:, 5:6], in1=bwk[:, 0:1], op=ALU.mult))
            nc.vector.tensor_tensor(out=bwk[:, 6:7], in0=gbt[:, 1:2], in1=bwk[:, 7:8],
                                    op=ALU.subtract).then_inc(s_bn5, 1)
            dve.wait_ge(s_bn5, 1)
            for dst, done in ((wx16, s_wx16), (wx, s_wx)):
                for k in range(4):
                    dve.wait_ge(s_y, k + 1)
                    nc.vector.tensor_scalar(dst[:, k * CW:(k + 1) * CW], WX_BANKS[k][:], bwk[:, 5:6], bwk[:, 6:7],
                                            ALU.mult, ALU.add).then_inc(done, 1)
            ya, yb = y32[(FULL_SWEEPS - 1) % 2], y32[FULL_SWEEPS % 2]
            ALL = 4 * (HALF_SWEEPS + FULL_SWEEPS)

            def out_add(k):
                dve.wait_ge(s_y, ALL + k + 1)
                nc.vector.tensor_tensor(out=outt[:, k * CW:(k + 1) * CW], in0=t2T[:, k * CW:(k + 1) * CW],
                                        in1=chunk(yb, k), op=ALU.add).then_inc(s_out, 1)

            def step_max(k):
                dve.wait_ge(s_df, k + 1)
                return nc.vector.tensor_reduce(out=dmax[:, k:k + 1], in_=diff[:, k * CW:(k + 1) * CW], axis=AX,
                                               op=ALU.max, apply_absolute_value=True)

            dve.wait_ge(s_wx, 4)
            for w in range(FULL_SWEEPS):
                for k in range(4):
                    dve.wait_ge(s_v, 4 * (HALF_SWEEPS + w) + k + 1)
                    if w:
                        dve.wait_ge(s_y, 4 * (HALF_SWEEPS + w) + k + 1)
                    nc.vector.tensor_tensor(out=zsw[:, k, :], in0=V_BANKS[k][:], in1=wx[:, k * CW:(k + 1) * CW],
                                            op=ALU.add).then_inc(s_z, 1)
                    if w == FULL_SWEEPS - 1 and k == 2:
                        out_add(0)
            step_max(0)
            for k in range(1, 4):
                out_add(k)
                ins = step_max(k)
            link(ins)
            nc.vector.reduce_max(dmax[:, 4:5], dmax[:, 0:4], AX).then_inc(s_dm, 1)
            dve.wait_ge(s_dmt, 1)
            link(nc.vector.reduce_max(dmax[0:1, 5:6], banks[4][0:1, 0:P], AX))
            nc.vector.tensor_scalar(flag[0:1, 0:1], dmax[0:1, 5:6], RESIDUAL_LIMIT, None, ALU.is_gt).then_inc(s_flag, 1)
            dve.wait_ge(s_flag, 1)
            f = dve.value_load(flag[0:1, 0:1], min_val=0, max_val=1)
            with dve.If(f > 0):
                nc.vector.memset(diff[:, 0:1], 0.0).then_inc(s_sy, 1)
                wx2 = wx[:].rearrange("p (a n) -> p a n", a=2)
                with dve.Fori(0, N) as t:
                    dve.wait_ge(s_sv, t + 1)
                    nc.vector.tensor_tensor(out=zseq[:], in0=banks[0][:, 0:2],
                                            in1=wx2[:, :, ds(t, 1)].rearrange("p a b -> p (a b)"),
                                            op=ALU.add).then_inc(s_sz, 1)
                dve.wait_ge(s_sy, N + 1)
                dve.wait_ge(s_store, 4 * 16)
                for k in range(4):
                    nc.vector.tensor_tensor(out=outt[:, k * CW:(k + 1) * CW], in0=t2T[:, k * CW:(k + 1) * CW],
                                            in1=chunk(yb, k), op=ALU.add).then_inc(s_out, 1)

        def pool_unit(ph, s, u, b, bprev, first, prev_first, has_prev, last=False):
            for n in range(ph.n):
                if n in ph.pool_items:
                    rest_item(nc.gpsimd, ph, s, u, n, first)
                for c in range(NC):
                    if n == add_slot(ph, c) - (HURRY if last else 0):
                        pool_add(ph, s, u, b, c, first)
                    if has_prev and n == add_slot(ph, c) - ph.n:
                        pool_add(ph, s, u - 1, bprev, c, prev_first)

        @block.gpsimd
        def _(pool):
            pool.wait_ge(s_w, 16)
            for i, t in enumerate((wqT, wkT, wvT)):
                shape = [P, H // 2, 2, C]
                nc.gpsimd.tensor_tensor(out=t[:].rearrange("p g (k c) -> p g k c", k=2),
                                        in0=aw[:, i].unsqueeze(2).to_broadcast(shape),
                                        in1=aw[:, i, :, 0:1].unsqueeze(2).to_broadcast(shape),
                                        op=ALU.subtract).then_inc(s_wt, 1)
            for b in range(1, B):
                pool.wait_ge(s_x[b], 32)
                pool.wait_ge(s_x16, b)
                nc.gpsimd.tensor_copy(x16[:, b * N:(b + 1) * N], xc[:, b * N:(b + 1) * N]).then_inc(s_xh, 1)
                pool.wait_ge(s_xh, b)
                nc.gpsimd.tensor_tensor(out=x16[C:P, b * N:(b + 1) * N], in0=xc[C:P, b * N:(b + 1) * N],
                                        in1=x16[C:P, b * N:(b + 1) * N], op=ALU.subtract).then_inc(s_x16, 1)
            pool.wait_ge(s_x16, B)
            pool.wait_ge(s_tok, 16)
            for u in range(B):
                pool_unit(CONV, cs, u, u, u - 1, u == 0, u == 1, u > 0)
            pool_add(CONV, cs, B - 1, B - 1, NC - 1, False)
            pool.wait_ge(cs.added, B * NC)
            pool_unit(ATTN, as_, 0, 0, 0, True, False, False)
            with pool.Fori(0, (UNITS - 2) // 2) as i:
                pool_unit(ATTN, as_, 1 + 2 * i, (1 + 2 * i) // H, (2 * i) // H, False, True, True)
                pool_unit(ATTN, as_, 2 + 2 * i, (2 + 2 * i) // H, (1 + 2 * i) // H, False, False, True)
            pool_unit(ATTN, as_, UNITS - 1, B - 1, B - 1, False, False, True, last=True)
            pool_add(ATTN, as_, UNITS - 1, B - 1, NC - 1, False)
            ya, yb = y32[(FULL_SWEEPS - 1) % 2], y32[FULL_SWEEPS % 2]
            for k in range(4):
                pool.wait_ge(s_y, 4 * (HALF_SWEEPS + FULL_SWEEPS) + k + 1)
                nc.gpsimd.tensor_tensor(out=diff[:, k * CW:(k + 1) * CW], in0=chunk(ya, k), in1=chunk(yb, k),
                                        op=ALU.subtract).then_inc(s_df, 1)

        def sp_maxrow(ph, s, u, par):
            nc.sync.wait_ge(s.prep_used, (u + 1) * ph.nprep)
            nc.sync.dma_start(q_hi[par][0:1, :], mrow[par][:]).then_inc(s.maxrow, 16)

        @block.sync
        def _(sp):
            sp.dma_start(cw[:], conv_w).then_inc(s_cw, 16)
            sp.dma_start(xc[0:C, 0:N], x_cm[0]).then_inc(s_x[0], 16)
            for b in range(1, B):
                for r in range(2):
                    sp.dma_start(xc[r * C:(r + 1) * C, b * N:(b + 1) * N], x_cm[b]).then_inc(s_x[b], 16)
            sp.dma_start(tok[:], x_tm).then_inc(s_tok, 16)
            sp.dma_start(cproj[:], conv_proj).then_inc(s_cproj, 16)
            sp.dma_start(ffn_w[:], ffn).then_inc(s_ffn, 16)
            sp.dma_start(gbt[:], gb).then_inc(s_ffn, 16)
            for u in range(B):
                sp_maxrow(CONV, cs, u, u % 2)
            sp_maxrow(ATTN, as_, 0, 0)
            with sp.Fori(0, (UNITS - 2) // 2) as i:
                sp_maxrow(ATTN, as_, 1 + 2 * i, 1)
                sp_maxrow(ATTN, as_, 2 + 2 * i, 0)
            sp_maxrow(ATTN, as_, UNITS - 1, 1)

            def store(k):
                sp.dma_start(out[(k // 2) * P:(k // 2 + 1) * P, (k % 2) * CW:(k % 2 + 1) * CW],
                             outt[:, k * CW:(k + 1) * CW]).then_inc(s_store, 16)

            for k in range(4):
                sp.wait_ge(s_out, k + 1)
                store(k)
            sp.wait_ge(s_store, 4 * 16)
            sp.wait_ge(s_flag, 1)
            f = sp.value_load(flag[0:1, 0:1], min_val=0, max_val=1)
            with sp.If(f > 0):
                for k in range(4):
                    sp.wait_ge(s_out, 4 + k + 1)
                    store(k)
                sp.wait_ge(s_store, 8 * 16)


def kernel(x, L0_conv_wq, L0_conv_wk, L0_conv_wv, L0_conv_wo, L1_attn_Wq, L1_attn_Wk, L1_attn_Wv, L1_attn_Wo,
           L1_ffn_W, L1_ffn_V, L1_ffn_gamma, L1_ffn_beta):
    import numpy as np
    import concourse.bacc as bacc
    from concourse.bass_utils import run_bass_kernel_spmd as run

    x = np.asarray(x)
    f = x.dtype
    x_cm = np.ascontiguousarray(x.reshape(B, C, N))
    x_tm = np.ascontiguousarray(x_cm.reshape(B, C, NT, P).transpose(3, 2, 0, 1).reshape(P, NT * B * C))
    conv_w = np.zeros((P, 3, P), f)
    for i, w in enumerate((L0_conv_wq, L0_conv_wk, L0_conv_wv)):
        conv_w[:, i, MC:2 * MC] = conv_w[:, i, 2 * MC:3 * MC] = np.tile(np.asarray(w).T, (2, 1))
    conv_proj = np.zeros((P, PO), f)
    conv_proj[MC:2 * MC, 0:C] = conv_proj[2 * MC:3 * MC, 0:C] = np.asarray(L0_conv_wo).T
    conv_proj[0, C] = 1.0
    attn_w = np.stack([w.reshape(H // 2, P, C).transpose(1, 0, 2) for w in
                       (np.asarray(L1_attn_Wq).T, np.asarray(L1_attn_Wk).T, np.asarray(L1_attn_Wv).T,
                        np.asarray(L1_attn_Wo))], axis=1)
    ffn = np.zeros((P, 2, P), f)
    for i, w in enumerate((L1_ffn_W, L1_ffn_V)):
        ffn[0:C, i, 0:C] = ffn[C:P, i, C:P] = np.asarray(w).T
    gb = np.stack([np.tile(np.asarray(L1_ffn_gamma), 2), np.tile(np.asarray(L1_ffn_beta), 2)], axis=1)
    const = np.zeros((P, CONST_COLS), f)
    r, c = np.arange(P)[:, None], np.arange(P)[None, :]
    const[:, K_IDENT:K_IDENT + P] = r == c
    const[:, K_AVG:K_AVG + P] = np.where(r % C == c % C, 0.5, 0.0)
    const[:, K_MASK_T:K_MASK_T + P] = np.where(c < r, NEG, 0.0)
    const[:, K_MASK_R:K_MASK_R + P] = np.where(c > r, NEG, 0.0)

    arrays = dict(x_cm=x_cm, x_tm=x_tm, conv_w=conv_w.reshape(P, 3 * P), conv_proj=conv_proj,
                  attn_w=attn_w.reshape(P, 4 * (H // 2) * C), ffn=ffn, gb=gb, const=const)
    arrays = {k: np.ascontiguousarray(v) for k, v in arrays.items()}
    nc = bacc.Bacc("TRN2", target_bir_lowering=False, num_devices=1)
    aps = {k: nc.dram_tensor(f"in_{k}", v.shape, mybir.dt.from_np(v.dtype), kind="ExternalInput").ap()
           for k, v in arrays.items()}
    out = nc.dram_tensor("out", (B * C, N), mybir.dt.float32, kind="ExternalOutput").ap()
    build(nc, out=out, **aps)
    res = run(nc, [{f"in_{k}": v for k, v in arrays.items()}], core_ids=[0])
    return res.results[0]["out"].reshape(x.shape)
```
